# Optimizing a Trainium2 kernel written in Bass

```python
import numpy as np
import jax
import jax.numpy as jnp

def _softmax(x, axis=-1):
    return jax.nn.softmax(x, axis=axis)

def _gelu(x):
    return jax.nn.gelu(x, approximate=True)

def _silu(x):
    return jax.nn.silu(x)

def _sigmoid(x):
    return jax.nn.sigmoid(x)

def _layernorm(x, axis=-1, eps=1e-05):
    m = jnp.mean(x, axis=axis, keepdims=True)
    v = jnp.var(x, axis=axis, keepdims=True)
    return (x - m) / jnp.sqrt(v + eps)

def _scatter_add(tgt, idx, src, axis=0):
    return tgt.at[idx].add(src)

def _segment_sum(src, seg, n):
    return jax.ops.segment_sum(src, seg, n)
kernel_name = 'mk_seq_preln_d1_jaxref_r8_9bf31f'

def setup_inputs(seed: int=0):
    np.random.seed(seed)
    _w = jnp.asarray

    def _L0_attn_setup():
        import jax, jax.numpy as jnp
        import numpy as np
        H, DK, DV, M = (8, 64, 64, 8)

        def _l2norm(x, eps=1e-06):
            return x * jax.lax.rsqrt(jnp.sum(x * x, axis=-1, keepdims=True) + eps)

        def _rotary(x, cos, sin):
            d = x.shape[-1] // 2
            x1, x2 = (x[..., :d], x[..., d:])
            c = cos[:, None]
            s = sin[:, None]
            return jnp.concatenate([x1 * c + x2 * s, -x1 * s + x2 * c], axis=-1)
        key = jax.random.key(seed)
        ks = jax.random.split(key, 11)
        B, T, D = (2, 256, 128)
        w = lambda k, shape, s=0.02: jax.random.normal(k, shape, jnp.float32) * s
        return {'hidden_states': jax.random.normal(ks[0], (B, T, D), jnp.float32), 'Wq': w(ks[1], (D, H * DK)), 'Wk': w(ks[2], (D, H * DK)), 'Wv': w(ks[3], (D, H * DV)), 'Wbeta': w(ks[4], (D, H * M)), 'Wtg': w(ks[5], (D, H * M)), 'mode_logits': w(ks[6], (H, M), 0.1), 'log_decay': w(ks[7], (H, M), 0.1), 'omega_log_scale': w(ks[8], (H, M), 0.1), 'Wg': w(ks[9], (D, H * DV)), 'Wo': w(ks[10], (H * DV, D))}
    _L0_attn_in = _L0_attn_setup()

    def _L0_ffn_setup():
        import jax, jax.numpy as jnp
        import numpy as np
        N_EXPERTS = 8
        N_GROUP = 4
        TOPK_GROUP = 2
        TOP_K = 2
        HIDDEN = 128
        INTER = 256
        B, S = (1, 128)

        def _grouped_topk(scores):
            T, E = scores.shape
            per_group = E // N_GROUP
            group_scores = scores.reshape(T, N_GROUP, per_group).max(-1)
            _, gidx = jax.lax.top_k(group_scores, TOPK_GROUP)
            gmask = jnp.zeros((T, N_GROUP), scores.dtype).at[jnp.arange(T)[:, None], gidx].set(1.0)
            smask = jnp.repeat(gmask, per_group, axis=1)
            masked = jnp.where(smask > 0, scores, 0.0)
            topk_w, topk_ids = jax.lax.top_k(masked, TOP_K)
            topk_w = topk_w / topk_w.sum(-1, keepdims=True)
            return (topk_ids, topk_w)
        key = jax.random.key(seed)
        k1, k2, k3, k4 = jax.random.split(key, 4)
        return {'hidden_states': jax.random.normal(k1, (B, S, HIDDEN), jnp.float32), 'gate_w': jax.random.normal(k2, (N_EXPERTS, HIDDEN), jnp.float32) * 0.02, 'w13_weight': jax.random.normal(k3, (N_EXPERTS, 2 * INTER, HIDDEN), jnp.float32) * 0.02, 'w2_weight': jax.random.normal(k4, (N_EXPERTS, HIDDEN, INTER), jnp.float32) * 0.02}
    _L0_ffn_in = _L0_ffn_setup()
    _d = {'L0_attn_hidden_states': _L0_attn_in['hidden_states'], 'L0_attn_Wq': _L0_attn_in['Wq'], 'L0_attn_Wk': _L0_attn_in['Wk'], 'L0_attn_Wv': _L0_attn_in['Wv'], 'L0_attn_Wbeta': _L0_attn_in['Wbeta'], 'L0_attn_Wtg': _L0_attn_in['Wtg'], 'L0_attn_mode_logits': _L0_attn_in['mode_logits'], 'L0_attn_log_decay': _L0_attn_in['log_decay'], 'L0_attn_omega_log_scale': _L0_attn_in['omega_log_scale'], 'L0_attn_Wg': _L0_attn_in['Wg'], 'L0_attn_Wo': _L0_attn_in['Wo'], 'L0_ffn_gate_w': _L0_ffn_in['gate_w'], 'L0_ffn_w13_weight': _L0_ffn_in['w13_weight'], 'L0_ffn_w2_weight': _L0_ffn_in['w2_weight']}
    _x0 = _d['L0_attn_hidden_states']
    _d['L0_attn_hidden_states'] = jax.random.normal(jax.random.fold_in(jax.random.key(seed), 1), (8, 512, 128), dtype=_x0.dtype)
    del _x0
    return _d

def reference(L0_attn_hidden_states, L0_attn_Wq, L0_attn_Wk, L0_attn_Wv, L0_attn_Wbeta, L0_attn_Wtg, L0_attn_mode_logits, L0_attn_log_decay, L0_attn_omega_log_scale, L0_attn_Wg, L0_attn_Wo, L0_ffn_gate_w, L0_ffn_w13_weight, L0_ffn_w2_weight):

    def _L0_attn_ref(hidden_states, Wq, Wk, Wv, Wbeta, Wtg, mode_logits, log_decay, omega_log_scale, Wg, Wo):
        import jax, jax.numpy as jnp
        import numpy as np
        H, DK, DV, M = (8, 64, 64, 8)

        def _l2norm(x, eps=1e-06):
            return x * jax.lax.rsqrt(jnp.sum(x * x, axis=-1, keepdims=True) + eps)

        def _rotary(x, cos, sin):
            d = x.shape[-1] // 2
            x1, x2 = (x[..., :d], x[..., d:])
            c = cos[:, None]
            s = sin[:, None]
            return jnp.concatenate([x1 * c + x2 * s, -x1 * s + x2 * c], axis=-1)
        x = hidden_states
        B, T, D = x.shape
        q = (x @ Wq).reshape(B, T, H, DK)
        k = (x @ Wk).reshape(B, T, H, DK)
        v = (x @ Wv).reshape(B, T, H, DV)
        beta = jax.nn.sigmoid((x @ Wbeta).reshape(B, T, H, M))
        tg = jax.nn.sigmoid((x @ Wtg).reshape(B, T, H, M))
        pair = jnp.arange(0, DK, 2, dtype=jnp.float32)
        inv_freq = 1.0 / 10000.0 ** (pair / DK)
        omega_scale = jnp.exp(omega_log_scale)
        pos = jnp.arange(T, dtype=jnp.float32)
        angles = pos[:, None, None, None] * omega_scale[None, :, :, None] * inv_freq
        cos = jnp.transpose(jnp.cos(angles), (2, 0, 1, 3))
        sin = jnp.transpose(jnp.sin(angles), (2, 0, 1, 3))
        scale = DK ** (-0.5)
        qr = _l2norm(_rotary(q, cos, sin)) * scale
        kr = _l2norm(_rotary(k, cos, sin))
        rho = jnp.exp(-jax.nn.softplus(log_decay))
        g = jnp.log(jnp.clip(tg * rho, 1e-06))
        qt = jnp.transpose(qr, (2, 0, 1, 3, 4))
        kt = jnp.transpose(kr, (2, 0, 1, 3, 4))
        vt = jnp.transpose(v, (1, 0, 2, 3))
        gt = jnp.transpose(g, (1, 3, 0, 2))
        bt = jnp.transpose(beta, (1, 3, 0, 2))

        def step(S, inp):
            q_t, k_t, v_t, b_g, b_beta = inp
            S = S * jnp.exp(b_g)[..., None, None]
            kv = jnp.einsum('mbhk,mbhkv->mbhv', k_t, S)
            dv = (v_t[None] - kv) * b_beta[..., None]
            S = S + k_t[..., :, None] * dv[..., None, :]
            o_t = jnp.einsum('mbhk,mbhkv->mbhv', q_t, S)
            return (S, o_t)
        S0 = jnp.zeros((M, B, H, DK, DV), jnp.float32)
        _, ys = jax.lax.scan(step, S0, (qt, kt, vt, gt, bt))
        mode_w = jax.nn.softmax(mode_logits, axis=-1)
        o = jnp.einsum('tmbhv,hm->bthv', ys, mode_w)
        gate = jax.nn.sigmoid((x @ Wg).reshape(B, T, H, DV))
        o = o * gate
        return o.reshape(B, T, H * DV) @ Wo

    def _L0_ffn_ref(hidden_states, gate_w, w13_weight, w2_weight):
        import jax, jax.numpy as jnp
        import numpy as np
        N_EXPERTS = 8
        N_GROUP = 4
        TOPK_GROUP = 2
        TOP_K = 2
        HIDDEN = 128
        INTER = 256
        B, S = (1, 128)

        def _grouped_topk(scores):
            T, E = scores.shape
            per_group = E // N_GROUP
            group_scores = scores.reshape(T, N_GROUP, per_group).max(-1)
            _, gidx = jax.lax.top_k(group_scores, TOPK_GROUP)
            gmask = jnp.zeros((T, N_GROUP), scores.dtype).at[jnp.arange(T)[:, None], gidx].set(1.0)
            smask = jnp.repeat(gmask, per_group, axis=1)
            masked = jnp.where(smask > 0, scores, 0.0)
            topk_w, topk_ids = jax.lax.top_k(masked, TOP_K)
            topk_w = topk_w / topk_w.sum(-1, keepdims=True)
            return (topk_ids, topk_w)
        Bm, Sm, H = hidden_states.shape
        x = hidden_states.reshape(-1, H)
        T = x.shape[0]
        scores = jax.nn.softmax(x @ gate_w.T, axis=-1)
        topk_ids, topk_w = _grouped_topk(scores)
        combine = jnp.zeros((T, N_EXPERTS), x.dtype).at[jnp.arange(T)[:, None], topk_ids].add(topk_w)
        gu = jnp.einsum('th,eih->tei', x, w13_weight)
        gate, up = (gu[..., :INTER], gu[..., INTER:])
        act = jax.nn.silu(gate) * up
        act = act * combine[:, :, None]
        out = jnp.einsum('tei,ehi->th', act, w2_weight)
        return out.reshape(Bm, Sm, H)
    x = L0_attn_hidden_states
    x = x + _L0_attn_ref(_layernorm(x, axis=-1), L0_attn_Wq, L0_attn_Wk, L0_attn_Wv, L0_attn_Wbeta, L0_attn_Wtg, L0_attn_mode_logits, L0_attn_log_decay, L0_attn_omega_log_scale, L0_attn_Wg, L0_attn_Wo)
    x = x + _L0_ffn_ref(_layernorm(x, axis=-1), L0_ffn_gate_w, L0_ffn_w13_weight, L0_ffn_w2_weight)
    return x

_drawn_inputs = setup_inputs


def setup_inputs(seed=0):
    import zlib

    import numpy as np

    out = dict(_drawn_inputs(seed))
    spreads = {}
    factors = {'L0_attn_Wq': 8.0,
     'L0_attn_Wk': 8.0,
     'L0_attn_Wv': 8.0,
     'L0_attn_Wbeta': 8.0,
     'L0_attn_Wtg': 8.0,
     'L0_attn_mode_logits': 8.0,
     'L0_attn_log_decay': 8.0,
     'L0_attn_omega_log_scale': 8.0,
     'L0_attn_Wg': 8.0,
     'L0_attn_Wo': 8.0,
     'L0_ffn_gate_w': 8.0,
     'L0_ffn_w13_weight': 8.0,
     'L0_ffn_w2_weight': 8.0}
    for name, (base, spread) in spreads.items():
        noise = np.random.default_rng([zlib.crc32(name.encode()), seed]).standard_normal(out[name].shape)
        drawn = base * np.exp(spread * noise) if base else spread * noise
        out[name] = jnp.asarray(drawn.astype(out[name].dtype))
    for name, factor in factors.items():
        out[name] = (out[name] * factor).astype(out[name].dtype)
    return out
```

```python
from contextlib import ExitStack

import concourse.bass as bass
from concourse import mybir

F32 = mybir.dt.float32
ALU = mybir.AluOpType
ACT = mybir.ActivationFunctionType
AX_X = mybir.AxisListType.X

B, T, D = 8, 512, 128
H, DK, DV, M = 8, 64, 64, 8
HALF = DK // 2
C = 32
NC = T // C
NSEQ = H * B
NT = T // 128
PAIRS = M // 2
SIDES = 2
QUADS = 4
UNITS = SIDES * NC
HM = H * M
E_X, GROUPS, INTER = 8, 4, 256
WIN = DK * 5 // 2
TWO_PI = 6.283185307179586
PI = 3.1415925
CW1 = 6.28125
CW2 = 0.0019350051879882812
CW3 = TWO_PI - CW1 - CW2
ROUND = 12582912.0
CLAMP = 44.0


class Chain:

    def __init__(self, eng, sem):
        self.eng, self.sem, self.n, self.seen = eng, sem, 0, 0

    def __call__(self, ins):
        ins.then_inc(self.sem, 1)
        self.n += 1
        return self.n

    def wait(self, n=None):
        n = self.n if n is None else n
        if n > self.seen:
            self.eng.wait_ge(self.sem, n)
            self.seen = n

    def link(self, ins):
        self(ins)
        self.wait()


def bcast(ap, axis, n):
    ap = ap.unsqueeze(axis)
    return ap.broadcast_to([*ap.shape[:axis], n, *ap.shape[axis + 1:]])


def program(nc, x, Wq, Wk, Wv, Wbeta, Wtg, mode_logits, log_decay, omega_log, Wg, Wo, gate_w, w13, w2,
            c_mat, c_pos, c_col, c_small, out):
    def dram(name, shape):
        return nc.dram_tensor(name, shape, F32, kind="Internal").ap()

    KQ_s = dram("KQ_s", (H, B, 128, NT, 2 * WIN))
    KV_s = dram("KV_s", (H, B, C, NC, 2 * DK))
    G_s = dram("G_s", (H, B, M, T))
    EG_s = dram("EG_s", (H, B, M, T))
    COL_s = dram("COL_s", (H, B, 128, 3, SIDES, NC))
    COSF_s = dram("COSF_s", (H, 128, PAIRS, T))
    SINF_s = dram("SINF_s", (H, 128, PAIRS, T))
    COST_s = dram("COST_s", (H, 128, SIDES, NC, HALF))
    SINT_s = dram("SINT_s", (H, 128, SIDES, NC, HALF))
    O_s = dram("O_s", (NSEQ, T, DV))

    with ExitStack() as whole:
        def keep(name, shape):
            return whole.enter_context(nc.sbuf_tensor(name, shape, F32))

        sems = [nc.alloc_semaphore(f"phase_{i}") for i in range(40)]
        first = sems[0].num
        assert [s.num for s in sems] == list(range(first, first + 40))

        def fresh():
            nc.all_engine_barrier(sems_to_clear=range(first, first + 40))

        ident = keep("ident", [128, 128])
        xnT = keep("xnT", [128, B * T])
        w_side = keep("w_side", [128, H, SIDES])
        w_pair = keep("w_pair", [128, H, PAIRS])

        prepare(nc, sems, fresh, x, Wq, Wk, Wv, Wbeta, Wtg, mode_logits, log_decay, omega_log,
                c_mat, c_pos, c_col, ident, xnT, w_side, w_pair,
                KQ_s, KV_s, G_s, EG_s, COL_s, COSF_s, SINF_s, COST_s, SINT_s)
        recurrence(nc, sems, fresh, c_mat, c_small, ident, w_side, w_pair,
                   KQ_s, KV_s, G_s, EG_s, COL_s, COSF_s, SINF_s, COST_s, SINT_s, O_s)
        experts(nc, sems, fresh, x, Wg, Wo, gate_w, w13, w2, c_small, ident, xnT, O_s, out)


def prepare(nc, sems, fresh, x, Wq, Wk, Wv, Wbeta, Wtg, mode_logits, log_decay, omega_log,
            c_mat, c_pos, c_col, ident, xnT, w_side, w_pair,
            KQ_s, KV_s, G_s, EG_s, COL_s, COSF_s, SINF_s, COST_s, SINT_s):
    with ExitStack() as ctx:
        def sb(name, shape):
            return ctx.enter_context(nc.sbuf_tensor("set_" + name, shape, F32))

        tri, ones_c = sb("tri", [128, 128]), sb("ones_c", [128, 128])
        wq, wk, wv = sb("wq", [128, H * DK]), sb("wk", [128, H * DK]), sb("wv", [128, H * DV])
        wbt = sb("wbt", [128, 2 * HM])
        rho, modes, om = sb("rho", [128, HM]), sb("modes", [128, H, M]), sb("om", [128, H, M])
        mx = sb("mx", [128, H])
        om_side, om_pair = sb("om_side", [128, H, SIDES]), sb("om_pair", [128, H, PAIRS])
        raw = sb("raw", [128, 3, B * NT, HM])
        loaded, dve_s = sems[0], sems[1]
        exp_in, exp_out, put = sems[2], sems[3], sems[4]

        with nc.Block() as block:
            @block.sync
            def _(sp):
                sp.dma_start(ident[:, :], c_mat[0]).then_inc(loaded, 16)
                sp.dma_start(tri[:, :], c_mat[1]).then_inc(loaded, 16)
                sp.dma_start(ones_c[:, :], c_mat[2]).then_inc(loaded, 16)
                sp.dma_start(rho[:, :], log_decay.rearrange("(a h) m -> a (h m)", a=1).broadcast_to([128, HM])).then_inc(loaded, 16)
                sp.dma_start(modes[:, :, :], bcast(mode_logits, 0, 128)).then_inc(loaded, 16)
                sp.dma_start(om[:, :, :], bcast(omega_log, 0, 128)).then_inc(loaded, 16)
                sp.dma_start(wbt[:, 0:HM], Wbeta).then_inc(loaded, 16)
                sp.dma_start(wbt[:, HM:], Wtg).then_inc(loaded, 16)
                sp.dma_start(wq[:, :], Wq).then_inc(loaded, 16)
                sp.dma_start(wk[:, :], Wk).then_inc(loaded, 16)
                sp.dma_start(wv[:, :], Wv).then_inc(loaded, 16)
                sp.wait_ge(loaded, 11 * 16)

            @block.scalar
            def _(act):
                act.wait_ge(loaded, 11 * 16)
                act.activation(rho[:, :], rho[:, :], ACT.Exp).then_inc(exp_out, 1)
                act.activation(om[:, :, :], om[:, :, :], ACT.Exp).then_inc(exp_out, 1)
                act.wait_ge(exp_in, 1)
                act.activation(modes[:, :, :], modes[:, :, :], ACT.Exp).then_inc(exp_out, 1)

            @block.vector
            def _(dve):
                v = Chain(dve, dve_s)
                dve.wait_ge(loaded, 11 * 16)
                v.link(dve.tensor_reduce(mx[:, :], modes[:, :, :], AX_X, ALU.max))
                dve.tensor_tensor(modes[:, :, :], modes[:, :, :], bcast(mx[:, :], 2, M), ALU.subtract).then_inc(exp_in, 1)
                dve.wait_ge(exp_out, 3)
                v.link(dve.tensor_reduce(mx[:, :], modes[:, :, :], AX_X, ALU.add))
                v.link(dve.reciprocal(mx[:, :], mx[:, :]))
                v.link(dve.tensor_tensor(modes[:, :, :], modes[:, :, :], bcast(mx[:, :], 2, M), ALU.mult))
                v.link(dve.tensor_scalar(rho[:, :], rho[:, :], 1.0, None, ALU.add))
                v.link(dve.reciprocal(rho[:, :], rho[:, :]))
                for q in range(QUADS):
                    rows = slice(32 * q, 32 * q + 32)
                    v(dve.tensor_copy(w_side[rows, :, :], modes[rows, :, q::QUADS]))
                    v(dve.tensor_copy(om_side[rows, :, :], om[rows, :, q::QUADS]))
                for e in range(2):
                    rows = slice(64 * e, 64 * e + 64)
                    v(dve.tensor_copy(w_pair[rows, :, :], modes[rows, :, e::2]))
                    v(dve.tensor_copy(om_pair[rows, :, :], om[rows, :, e::2]))
                v.wait()
        fresh()

        project(nc, sems, fresh, x, wq, wk, wv, wbt, rho, tri, ones_c, ident, xnT, raw, KQ_s, KV_s, G_s, EG_s)

        with ExitStack() as part:
            cols = part.enter_context(nc.sbuf_tensor("cols", [128, NSEQ, 3, SIDES, NC], F32))
            with nc.Block() as block:
                def move(eng, done, arr):
                    for c4 in range(QUADS):
                        for q in range(QUADS):
                            for s in range(SIDES):
                                src = raw[32 * c4:32 * c4 + 32, arr, :, QUADS * s + q::M].rearrange(
                                    "t (b i) h -> t h b i", i=NT)
                                dst = cols[32 * q:32 * q + 32, :, arr, s, c4::QUADS].rearrange(
                                    "t (h b) i -> t h b i", b=B)
                                eng(dst, src).then_inc(done, 1)

                @block.vector
                def _(dve):
                    move(dve.tensor_copy, dve_s, 0)

                @block.scalar
                def _(act):
                    move(act.copy, exp_out, 1)

                @block.gpsimd
                def _(pool):
                    move(pool.tensor_copy, exp_in, 2)

                @block.sync
                def _(sp):
                    for done in (dve_s, exp_out, exp_in):
                        sp.wait_ge(done, QUADS * QUADS * SIDES)
                    sp.dma_start(COL_s.rearrange("h b p a s c -> p (h b) (a s c)"),
                                 cols[:, :, :, :, :].rearrange("p n a s c -> p n (a s c)")).then_inc(put, 16)
                    sp.wait_ge(put, 16)
            fresh()

        tables(nc, sems, fresh, c_pos, c_col, om_side, om_pair, COSF_s, SINF_s, COST_s, SINT_s)


def project(nc, sems, fresh, x, wq, wk, wv, wbt, rho, tri, ones_c, ident, xnT, raw, KQ_s, KV_s, G_s, EG_s):
    with ExitStack() as ctx:
        def sb(name, shape):
            return ctx.enter_context(nc.sbuf_tensor("proj_" + name, shape, F32))

        def ps(name, shape):
            return ctx.enter_context(nc.psum_tensor("proj_" + name, shape, F32))

        xs = sb("xs", [128, NT, D])
        sq = sb("sq", [128, NT, D])
        stat = sb("stat", [128, NT])
        std = sb("std", [128, NT])
        xT = sb("xT", [128, T])
        qk = sb("qk", [128, 2, NT, H * DK])
        sqq = sb("sqq", [128, 2, H * DK])
        ssq = sb("ssq", [128, 2, NT, H])
        win = sb("win", [128, NT, H, 2 * WIN])
        kv = sb("kv", [128, NT, H, 2 * DK])
        z = sb("z", [128, NT, 2 * HM])
        ez = sb("ez", [128, NT, 2 * HM])
        g = sb("g", [128, NT, HM])
        ex = sb("ex", [128, NT, HM])
        gt, egt = sb("gt", [HM, T]), sb("egt", [HM, T])
        bank = [ps(f"bank{i}", [128, 512]) for i in range(8)]
        (loaded, dve_s, act_s, pool_s, std_in, std_out, xn_done, xt_done, xt_copied, proj, freed_q, freed_k,
         freed_v, freed_z, logs_in, logs_out, g_done, sums, exp_in, exp_out, gt_done, scaled, put, kv_done) = sems[:24]

        DVE_BEFORE, DVE_TILE = 7, 2
        with nc.Fori(0, B) as b:
            with nc.Block() as block:
                @block.sync
                def _(sp):
                    sp.dma_start(xs[:, :, :], x[bass.ds(b, 1)].rearrange("a (i p) d -> p (a i) d", p=128)).then_inc(loaded, 16)
                    n = 0
                    sp.wait_ge(kv_done, 1)
                    for i in range(NT):
                        for c4 in range(QUADS):
                            sp.dma_start(KV_s[:, bass.ds(b, 1), :, QUADS * i + c4, :].rearrange("h a t e -> t (h a) e"),
                                         kv[32 * c4:32 * c4 + 32, i, :, :]).then_inc(put, 16)
                            n += 1
                    sp.wait_ge(gt_done, 2)
                    for h in range(H):
                        sp.dma_start(G_s[h, bass.ds(b, 1)].rearrange("a m t -> (a m) t"), gt[M * h:M * h + M, :]).then_inc(put, 16)
                        sp.dma_start(EG_s[h, bass.ds(b, 1)].rearrange("a m t -> (a m) t"), egt[M * h:M * h + M, :]).then_inc(put, 16)
                        n += 2
                    sp.wait_ge(scaled, 3)
                    for i in range(NT):
                        sp.dma_start(KQ_s[:, bass.ds(b, 1), :, i, :].rearrange("h a p e -> p (h a) e"), win[:, i, :, :]).then_inc(put, 16)
                        n += 1
                    sp.wait_ge(put, 16 * n)

                @block.tensor
                def _(pe):
                    pe.wait_ge(xn_done, 1)
                    for i in range(NT):
                        last = pe.transpose(bank[0][:, 128 * i:128 * i + 128], xs[:, i, :], ident[:, :])
                    last.then_inc(xt_done, 1)
                    for i in range(NT):
                        pe.wait_ge(xt_copied, 1)
                        if i >= 2:
                            pe.wait_ge(freed_q, 2 * (i - 1))
                            pe.wait_ge(freed_k, i - 1)
                            pe.wait_ge(freed_v, i - 1)
                            pe.wait_ge(freed_z, i - 1)
                        lhsT = xT[:, 128 * i:128 * i + 128]
                        o = 4 * (i % 2)
                        pe.matmul(bank[o][:, :], lhsT, wq[:, :], start=True, stop=True)
                        pe.matmul(bank[o + 1][:, :], lhsT, wk[:, :], start=True, stop=True)
                        pe.matmul(bank[o + 2][:, :], lhsT, wv[:, :], start=True, stop=True)
                        pe.matmul(bank[o + 3][:, 0:2 * HM], lhsT, wbt[:, :], start=True, stop=True).then_inc(proj, 1)
                    pe.wait_ge(g_done, 1)
                    pe.wait_ge(freed_q, 2 * NT)
                    pe.wait_ge(freed_k, NT)
                    pe.wait_ge(freed_v, NT)
                    for i in range(NT):
                        pe.matmul(bank[0][:, HM * i:HM * i + HM], tri[:, :], g[:, i, :], start=True, stop=True)
                    for i in range(NT):
                        pe.matmul(bank[1][:, HM * i:HM * i + HM], ones_c[:, :], g[:, i, :], start=True, stop=True)
                    for i in range(NT):
                        last = pe.matmul(bank[2][0:HM, 128 * i:128 * i + 128], g[:, i, :], tri[:, :], start=True, stop=True)
                    last.then_inc(sums, 1)

                @block.scalar
                def _(act):
                    a = Chain(act, act_s)
                    act.wait_ge(std_in, 1)
                    act.activation(std[:, :], std[:, :], ACT.Sqrt).then_inc(std_out, 1)
                    act.wait_ge(xt_done, 1)
                    act.copy(xT[:, :], bank[0][:, :]).then_inc(xt_copied, 1)
                    act.wait_ge(xt_copied, 1)
                    act.copy(xnT[:, bass.ds(b * T, T)], xT[:, :]).then_inc(pool_s, 1)
                    for i in range(NT):
                        o = 4 * (i % 2)
                        act.wait_ge(proj, i + 1)
                        if i:
                            act.wait_ge(dve_s, DVE_BEFORE + DVE_TILE * i)
                        act.copy(qk[:, 0, i, :], bank[o][:, :]).then_inc(freed_q, 1)
                        act.activation(sqq[:, 0, :], bank[o][:, :], ACT.Square).then_inc(freed_q, 1)
                        act.copy(qk[:, 1, i, :], bank[o + 1][:, :])\
                           .then_inc(act_s, 1)
                        act.activation(sqq[:, 1, :], bank[o + 1][:, :], ACT.Square).then_inc(freed_k, 1)
                        act.copy(kv[:, i, :, DK:], bank[o + 2][:, :].rearrange("p (h d) -> p h d", h=H)).then_inc(freed_v, 1)
                    act.wait_ge(std_in, 2)
                    act.activation(ssq[:, :, :, :], ssq[:, :, :, :], ACT.Sqrt).then_inc(std_out, 1)
                    act.wait_ge(logs_in, 1)
                    act.activation(ez[:, :, :], z[:, :, :], ACT.Exp, scale=-1.0).then_inc(logs_out, 1)
                    act.wait_ge(logs_in, 2)
                    act.activation(z[:, :, 0:HM], ez[:, :, 0:HM], ACT.Ln).then_inc(logs_out, 1)
                    act.activation(g[:, :, :], z[:, :, HM:], ACT.Ln).then_inc(g_done, 1)
                    act.wait_ge(sums, 1)
                    act.copy(gt[:, :], bank[2][0:HM, :]).then_inc(gt_done, 1)
                    act.wait_ge(gt_done, 1)
                    act.activation(egt[:, :], gt[:, :], ACT.Exp).then_inc(gt_done, 1)
                    act.wait_ge(exp_in, 1)
                    act.activation(ex[:, :, :], raw[:, 1, bass.ds(b * NT, NT), :], ACT.Exp).then_inc(exp_out, 1)
                    act.wait_ge(exp_in, 2)
                    act.activation(raw[:, 2, bass.ds(b * NT, NT), :], raw[:, 2, bass.ds(b * NT, NT), :], ACT.Exp).then_inc(exp_out, 1)
                    act.wait_ge(exp_out, 2)

                @block.vector
                def _(dve):
                    v = Chain(dve, dve_s)
                    dve.wait_ge(loaded, 16)
                    v.link(dve.tensor_reduce(stat[:, :], xs[:, :, :], AX_X, ALU.add))
                    v.link(dve.tensor_scalar(stat[:, :], stat[:, :], 1.0 / D, None, ALU.mult))
                    v.link(dve.tensor_tensor(xs[:, :, :], xs[:, :, :], bcast(stat[:, :], 2, D), ALU.subtract))
                    v.link(dve.tensor_tensor(sq[:, :, :], xs[:, :, :], xs[:, :, :], ALU.mult))
                    v.link(dve.tensor_reduce(stat[:, :], sq[:, :, :], AX_X, ALU.add))
                    dve.tensor_scalar(std[:, :], stat[:, :], 1.0 / D, 1e-5, ALU.mult, ALU.add).then_inc(std_in, 1)
                    dve.wait_ge(std_out, 1)
                    v.link(dve.reciprocal(std[:, :], std[:, :]))
                    dve.tensor_tensor(xs[:, :, :], xs[:, :, :], bcast(std[:, :], 2, D), ALU.mult).then_inc(xn_done, 1)
                    v.link(dve.memset(stat[:, :], 0.0))
                    assert v.n == DVE_BEFORE
                    for i in range(NT):
                        o = 4 * (i % 2)
                        dve.wait_ge(proj, i + 1)
                        dve.tensor_copy(z[:, i, :], bank[o + 3][:, 0:2 * HM]).then_inc(freed_z, 1)
                        dve.wait_ge(freed_q, 2 * i + 2)
                        v(dve.tensor_reduce(ssq[:, 0, i, :], sqq[:, 0, :].rearrange("p (h d) -> p h d", h=H), AX_X, ALU.add))
                        dve.wait_ge(freed_k, i + 1)
                        v(dve.tensor_reduce(ssq[:, 1, i, :], sqq[:, 1, :].rearrange("p (h d) -> p h d", h=H), AX_X, ALU.add))
                    v.wait()
                    dve.tensor_scalar(ssq[:, :, :, :], ssq[:, :, :, :], 1e-6, None, ALU.add).then_inc(std_in, 1)
                    dve.wait_ge(freed_z, NT)
                    dve.tensor_scalar(z[:, :, :], z[:, :, :], -CLAMP, None, ALU.max).then_inc(logs_in, 1)
                    dve.wait_ge(std_out, 2)
                    v.link(dve.reciprocal(ssq[:, :, :, :], ssq[:, :, :, :]))
                    v.link(dve.tensor_scalar(ssq[:, 0, :, :], ssq[:, 0, :, :], DK ** -0.5, None, ALU.mult))
                    dve.wait_ge(logs_out, 1)
                    v.link(dve.tensor_scalar(ez[:, :, :], ez[:, :, :], 1.0, None, ALU.add))
                    v.link(dve.reciprocal(z[:, :, HM:], ez[:, :, HM:]))
                    v.link(dve.tensor_tensor(z[:, :, HM:], z[:, :, HM:], bcast(rho[:, :], 1, NT), ALU.mult))
                    dve.tensor_scalar(z[:, :, HM:], z[:, :, HM:], 1e-6, None, ALU.max).then_inc(logs_in, 1)
                    dve.wait_ge(act_s, NT)
                    dve.wait_ge(freed_v, NT)
                    for i in range(NT):
                        last = dve.tensor_tensor(kv[:, i, :, 0:DK], qk[:, 1, i, :].rearrange("p (h d) -> p h d", h=H),
                                                 bcast(ssq[:, 1, i, :], 2, DK), ALU.mult)
                        if i < NT - 1:
                            v(last)
                        else:
                            last.then_inc(kv_done, 1)
                    for i in range(NT):
                        v(dve.tensor_tensor(win[:, i, :, WIN:WIN + DK], qk[:, 0, i, :].rearrange("p (h d) -> p h d", h=H),
                                            bcast(ssq[:, 0, i, :], 2, DK), ALU.mult))
                    v.wait()
                    for i in range(NT):
                        last = dve.tensor_copy(win[:, i, :, WIN + DK:WIN + 2 * DK], win[:, i, :, WIN:WIN + DK])
                        if i < NT - 1:
                            v(last)
                        else:
                            last.then_inc(scaled, 1)
                    dve.wait_ge(sums, 1)
                    dve.wait_ge(logs_out, 2)
                    G = bank[0][:, 0:NT * HM].rearrange("p (i m) -> p i m", i=NT)
                    G_end = bank[1][:, 0:NT * HM].rearrange("p (i m) -> p i m", i=NT)
                    here = bass.ds(b * NT, NT)
                    v.link(dve.scalar_tensor_tensor(out=raw[:, 0, here, :], in0=z[:, :, 0:HM], scalar=-1.0, in1=G,
                                                    op0=ALU.mult, op1=ALU.subtract))
                    dve.tensor_copy(raw[:, 1, here, :], G).then_inc(exp_in, 1)
                    dve.tensor_tensor(raw[:, 2, here, :], raw[:, 0, here, :], G_end, ALU.add).then_inc(exp_in, 1)
                    dve.wait_ge(exp_out, 1)
                    v.link(dve.tensor_scalar(raw[:, 1, here, :], ex[:, :, :], -1.0, None, ALU.mult))

                @block.gpsimd
                def _(pool):
                    pool.wait_ge(kv_done, 1)
                    for i in range(NT):
                        last = pool.tensor_copy(win[:, i, :, 0:DK], kv[:, i, :, 0:DK])
                        last = pool.tensor_copy(win[:, i, :, DK:2 * DK], kv[:, i, :, 0:DK])
                        last = pool.tensor_copy(win[:, i, :, 2 * DK:WIN], kv[:, i, :, 0:HALF])
                    last.then_inc(scaled, 1)
                    pool.wait_ge(scaled, 2)
                    for i in range(NT):
                        last = pool.tensor_copy(win[:, i, :, WIN + 2 * DK:], win[:, i, :, WIN:WIN + HALF])
                    last.then_inc(scaled, 1)
            fresh()


def tables(nc, sems, fresh, c_pos, c_col, om_side, om_pair, COSF_s, SINF_s, COST_s, SINT_s):
    NF, NTOK = PAIRS * T, SIDES * NC * HALF
    with ExitStack() as ctx:
        def sb(name, shape):
            return ctx.enter_context(nc.sbuf_tensor("tab_" + name, shape, F32))

        pos = sb("pos", [128, T])
        pos_c, freq_row = sb("pos_c", [128, NC]), sb("freq_row", [128, HALF])
        col = sb("col", [128, 4])
        pc = sb("pc", [128, SIDES, NC])
        om_now = sb("om_now", [128, SIDES + PAIRS])
        ang = sb("ang", [128, NF + NTOK])
        turns = sb("turns", [128, NF + NTOK])
        sin, cos = sb("sin", [128, NF + NTOK]), sb("cos", [128, NF + NTOK])
        loaded, dve_s, reduced, act_s, done, put = sems[:6]
        with nc.Block() as block:
            @block.sync
            def _(sp):
                sp.dma_start(pos[:, :], c_pos[:, 0:T]).then_inc(loaded, 16)
                sp.dma_start(pos_c[:, :], c_pos[:, T:T + NC]).then_inc(loaded, 16)
                sp.dma_start(freq_row[:, :], c_pos[:, T + NC:T + NC + HALF]).then_inc(loaded, 16)
                sp.dma_start(col[:, :], c_col).then_inc(loaded, 16)
                sp.wait_ge(loaded, 64)
        fresh()
        with nc.Fori(0, H) as h:
            with nc.Block() as block:
                @block.vector
                def _(dve):
                    v = Chain(dve, dve_s)
                    v(dve.tensor_copy(om_now[:, 0:SIDES], om_side[:, bass.ds(h, 1), :].rearrange("p a s -> p (a s)")))
                    v.link(dve.tensor_copy(om_now[:, SIDES:], om_pair[:, bass.ds(h, 1), :].rearrange("p a s -> p (a s)")))
                    for p in range(PAIRS):
                        v(dve.tensor_scalar(ang[:, T * p:T * p + T], pos[:, :], om_now[:, SIDES + p:SIDES + p + 1], col[:, 0:1],
                                            ALU.mult, ALU.mult))
                    for s in range(SIDES):
                        v(dve.tensor_scalar(pc[:, s, :], pos_c[:, :], om_now[:, s:s + 1], None, ALU.mult))
                    v.wait()
                    for s in range(SIDES):
                        half = ang[:, NF + s * NC * HALF:NF + (s + 1) * NC * HALF].rearrange("p (c j) -> p c j", c=NC)
                        v(dve.tensor_tensor(half, bcast(pc[:, s, :], 2, HALF), bcast(freq_row[:, :], 1, NC), ALU.mult))
                    v.wait()
                    v.link(dve.tensor_scalar(turns[:, :], ang[:, :], 1.0 / TWO_PI, ROUND, ALU.mult, ALU.add))
                    v.link(dve.tensor_scalar(turns[:, :], turns[:, :], ROUND, None, ALU.subtract))
                    for part in (CW1, CW2, CW3):
                        v.link(dve.scalar_tensor_tensor(out=ang[:, :], in0=turns[:, :], scalar=-part, in1=ang[:, :],
                                                        op0=ALU.mult, op1=ALU.add))
                    dve.tensor_scalar(ang[:, :], ang[:, :], PI, -PI, ALU.min, ALU.max).then_inc(reduced, 1)

                @block.scalar
                def _(act):
                    act.wait_ge(reduced, 1)
                    act.activation(sin[:, 0:NF], ang[:, 0:NF], ACT.Sin, scale=col[:, 1:2]).then_inc(done, 1)
                    act.activation(sin[:, NF:], ang[:, NF:], ACT.Sin).then_inc(done, 1)
                    act.activation(turns[:, :], ang[:, :], ACT.Abs).then_inc(act_s, 1)
                    act.wait_ge(act_s, 1)
                    act.activation(cos[:, :], turns[:, :], ACT.Sin, scale=-1.0, bias=col[:, 2:3]).then_inc(done, 1)

                @block.sync
                def _(sp):
                    sp.wait_ge(done, 2)
                    sp.dma_start(SINF_s[bass.ds(h, 1)].rearrange("a p e t -> (a p) (e t)"), sin[:, 0:NF]).then_inc(put, 16)
                    sp.dma_start(SINT_s[bass.ds(h, 1)].rearrange("a p s c j -> (a p) (s c j)"), sin[:, NF:]).then_inc(put, 16)
                    sp.wait_ge(done, 3)
                    sp.dma_start(COSF_s[bass.ds(h, 1)].rearrange("a p e t -> (a p) (e t)"), cos[:, 0:NF]).then_inc(put, 16)
                    sp.dma_start(COST_s[bass.ds(h, 1)].rearrange("a p s c j -> (a p) (s c j)"), cos[:, NF:]).then_inc(put, 16)
                    sp.wait_ge(put, 64)
            fresh()


def recurrence(nc, sems, fresh, c_mat, c_small, ident, w_side, w_pair,
               KQ_s, KV_s, G_s, EG_s, COL_s, COSF_s, SINF_s, COST_s, SINT_s, O_s):
    with ExitStack() as ctx:
        def sb(name, shape):
            return ctx.enter_context(nc.sbuf_tensor("run_" + name, shape, F32))

        def ps(name, shape):
            return ctx.enter_context(nc.psum_tensor("run_" + name, shape, F32))

        KQ = sb("KQ", [128, 3, PAIRS, T])
        Qd = sb("Qd", [128, 2, PAIRS, T])
        XT = sb("XT", [128, 2, SIDES, NC, C])
        PT = sb("PT", [128, 2, SIDES, NC, C])
        KD = sb("KD", [128, 2, SIDES, NC, DK])
        KV = sb("KV", [128, 2, NC, 2 * DK])
        col = sb("col", [128, 2, 3, SIDES, NC])
        decay = sb("decay", [128, 2, PAIRS, NC])
        win = sb("win", [128, NT, 2 * WIN])
        GR = sb("GR", [128, SIDES, T])
        EG = sb("EG", [128, PAIRS, T])
        DB = sb("DB", [128, SIDES, NC, C])
        kqT = sb("kqT", [128, 4, T])
        cosF, sinF = sb("cosF", [128, PAIRS, T]), sb("sinF", [128, PAIRS, T])
        cosT, sinT = sb("cosT", [128, SIDES, NC, HALF]), sb("sinT", [128, SIDES, NC, HALF])
        tmpv, tmpg = sb("tmpv", [128, PAIRS, 128]), sb("tmpg", [128, PAIRS, 128])
        turned = sb("turned", [128, NC, 2, HALF])
        AT = sb("AT", [128, SIDES, NC, C])
        AL, XL, EL = sb("AL", [128, C, C]), sb("XL", [128, C, C]), sb("EL", [128, C * C])
        below, eye = sb("below", [128, C]), sb("eye", [128, C * C])
        S = sb("S", [128, 2, PAIRS, DV])
        R = sb("R", [128, SIDES, DV])
        W = sb("W", [128, SIDES, DV])
        O = sb("O", [128, 2, NT, DV])
        RW = [ps(f"RW{s}", [128, 512]) for s in range(SIDES)]
        SB = [ps(f"SB{s}", [128, 512]) for s in range(SIDES)]
        OB = [ps(f"OB{s}", [128, NT, 128]) for s in range(2)]
        prep = [ps(f"prep{s}", [128, 512]) for s in range(2)]

        (l_win, l_gr, l_eg, l_col, l_kv, l_tab, pe_t, act_t, rot_k, rot_q, pe_s, d_ready, d_exp, scored,
         pool_s, dve_s, qd_done, xt_done, kd_done, pe_o, act_o, stored, tab_used) = sems[:23]
        pe_r, dve_r = sems[23:25], sems[25:27]
        pe_w, act_w = sems[27:29], sems[29:31]
        pe_f, dve_f = sems[31:33], sems[33:35]
        l_const, l_tok = sems[35:37]
        with nc.Block() as block:
            @block.sync
            def _(sp):
                sp.dma_start(below[:, :], c_mat[3, :, 0:C]).then_inc(l_const, 16)
                sp.dma_start(eye[:, :], c_small[0:1, 0:C * C].broadcast_to([128, C * C])).then_inc(l_const, 16)
                sp.wait_ge(l_const, 32)
        fresh()

        def pair_of(s, q):
            return 2 * s + q // 2

        def emit(n0, odd, steps):
            with nc.Block() as block:
                @block.sync
                def _(sp):
                    prepared = 0
                    for k, (runs, prepares) in enumerate(steps):
                        if prepares:
                            n = n0 + (k + 1)
                            par = (odd + k + 1) % 2
                            a = prepared
                            if runs and k:
                                sp.wait_ge(pe_o, NC * k)
                            if a:
                                sp.wait_ge(pe_t, 4 * a)
                            sp.dma_start(win[:, :, :], KQ_s.rearrange("h b p i e -> (h b) p i e")[bass.ds(n, 1)].rearrange("a p i e -> p (a i) e")).then_inc(l_win, 16)
                            sp.dma_start(col[:, par], COL_s.rearrange("h b p k s c -> (h b) p k s c")[bass.ds(n, 1)].rearrange("a p k s c -> (a p) k s c")).then_inc(l_col, 16)
                            if a:
                                sp.wait_ge(pool_s, POOL_GR + POOL_STEP * (a - 1))
                            for q in range(QUADS):
                                sp.dma_start(GR[32 * q:32 * q + 32],
                                             G_s.rearrange("h b m t -> (h b) m t")[bass.ds(n, 1), q::QUADS, :].broadcast_to([32, SIDES, T])).then_inc(l_gr, 16)
                            if a:
                                sp.wait_ge(rot_k, NT * a)
                                sp.wait_ge(rot_q, NT * a)
                                sp.wait_ge(kd_done, a)
                            h = n // B
                            sp.dma_start(cosF[:, :, :], COSF_s[bass.ds(h, 1)].rearrange("a p e t -> (a p) e t")).then_inc(l_tab, 16)
                            sp.dma_start(sinF[:, :, :], SINF_s[bass.ds(h, 1)].rearrange("a p e t -> (a p) e t")).then_inc(l_tab, 16)
                            for q in range(QUADS):
                                sp.dma_start(KV[32 * q:32 * q + 32, par],
                                             KV_s.rearrange("h b t c e -> (h b) t c e")[bass.ds(n, 1)].rearrange("a t c e -> (a t) c e")).then_inc(l_kv, 16)
                            sp.dma_start(cosT[:, :, :, :], COST_s[bass.ds(h, 1)].rearrange("a p s c j -> (a p) s c j")).then_inc(l_tok, 16)
                            sp.dma_start(sinT[:, :, :, :], SINT_s[bass.ds(h, 1)].rearrange("a p s c j -> (a p) s c j")).then_inc(l_tok, 16)
                            if a:
                                sp.wait_ge(qd_done, 2 * a)
                            for e in range(2):
                                sp.dma_start(EG[64 * e:64 * e + 64],
                                             EG_s.rearrange("h b m t -> (h b) m t")[bass.ds(n, 1), e::2, :].broadcast_to([64, PAIRS, T])).then_inc(l_eg, 16)
                            prepared += 1
                        if runs:
                            sp.wait_ge(act_o, k + 1)
                            sp.dma_start(O_s[bass.ds(n0 + k, 1)].rearrange("a (i p) v -> p (a i) v", p=128), O[:, k % 2]).then_inc(stored, 16)
                    if any(r for r, _ in steps):
                        sp.wait_ge(stored, 16 * sum(r for r, _ in steps))

                @block.gpsimd
                def _(pool):
                    g = Chain(pool, pool_s)
                    prepared = 0
                    for k, (runs, prepares) in enumerate(steps):
                        if not prepares:
                            continue
                        par = (odd + k + 1) % 2
                        a = prepared
                        start = g.n
                        pool.wait_ge(l_gr, 64 * (a + 1))
                        if a:
                            pool.wait_ge(scored, 2 * NT * a)
                        GRc = GR[:, :, :].rearrange("p s (c i) -> p (s c) i", i=C)
                        DBc = DB[:, :, :, :].rearrange("p s c i -> p (s c) i")
                        g.link(pool.tensor_tensor(DBc, GRc, bcast(below[:, :], 1, UNITS), ALU.add))
                        assert g.n == start + POOL_GR
                        pool.wait_ge(l_col, 16 * (a + 1))
                        colc = col[:, par, 0].rearrange("p s c -> p (s c)")
                        pool.tensor_tensor(DBc, DBc, bcast(colc, 2, C), ALU.add).then_inc(d_ready, 1)
                        pool.wait_ge(l_tab, 32 * (a + 1))
                        for i in range(NT):
                            t = slice(128 * i, 128 * i + 128)
                            if i == 0:
                                pool.wait_ge(act_t, 4 * a + 4)
                                if a:
                                    pool.wait_ge(qd_done, 2 * a)
                            g(pool.tensor_tensor(KQ[:, 2, :, t], cosF[:, :, t], bcast(kqT[:, 2, t], 1, PAIRS), ALU.mult))
                            g.link(pool.tensor_tensor(tmpg[:, :, :], sinF[:, :, t], bcast(kqT[:, 3, t], 1, PAIRS), ALU.mult))
                            pool.tensor_tensor(KQ[:, 2, :, t], KQ[:, 2, :, t], tmpg[:, :, :], ALU.add).then_inc(rot_q, 1)
                            pool.wait_ge(rot_q, NT * a + i + 1)
                        pool.wait_ge(l_tok, 32 * (a + 1))
                        pool.wait_ge(l_kv, 64 * (a + 1))
                        if runs and k:
                            pool.wait_ge(pe_o, NC * k)
                        kt = KV[:, par, :, 0:DK].rearrange("p c (z j) -> p c z j", z=2)
                        for s in range(SIDES):
                            kd = KD[:, par, s].rearrange("p c (z j) -> p c z j", z=2)
                            for z in range(2):
                                g(pool.tensor_tensor(kd[:, :, z, :], kt[:, :, z, :], cosT[:, s], ALU.mult))
                                g(pool.tensor_tensor(turned[:, :, z, :], kt[:, :, z, :], sinT[:, s], ALU.mult))
                            g.wait()
                            g(pool.tensor_tensor(kd[:, :, 0, :], kd[:, :, 0, :], turned[:, :, 1, :], ALU.add))
                            g.link(pool.tensor_tensor(kd[:, :, 1, :], kd[:, :, 1, :], turned[:, :, 0, :], ALU.subtract))
                            last = pool.tensor_tensor(KD[:, par, s], KD[:, par, s], bcast(col[:, par, 2, s, :], 2, DK), ALU.mult)
                            if s < SIDES - 1:
                                g.link(last)
                            else:
                                last.then_inc(kd_done, 1)
                        assert g.n == start + POOL_STEP
                        prepared += 1

                @block.scalar
                def _(act):
                    prepared = ran = 0
                    for k, (runs, prepares) in enumerate(steps):
                        a = prepared

                        def transposed(r):
                            act.wait_ge(pe_t, 4 * a + r + 1)
                            if r == 0 and a:
                                act.wait_ge(rot_k, NT * a)
                                act.wait_ge(rot_q, NT * a)
                            act.copy(kqT[:, r, :], prep[r % 2][:, :]).then_inc(act_t, 1)

                        def exponential():
                            act.wait_ge(d_ready, a + 1)
                            act.activation(DB[:, :, :, :], DB[:, :, :, :], ACT.Exp).then_inc(d_exp, 1)

                        jobs = [lambda r=r: transposed(r) for r in range(4)] + [exponential] if prepares else []
                        if not runs:
                            for job in jobs:
                                job()
                        else:
                            for c in range(NC):
                                for s in range(SIDES):
                                    act.wait_ge(pe_w[s], NC * k + c + 1)
                                    act.copy(W[:, s, :], RW[s][:, DV:2 * DV]).then_inc(act_w[s], 1)
                                for _ in range(2 if c < 2 else 1):
                                    if jobs:
                                        jobs.pop(0)()
                            act.wait_ge(pe_o, NC * (k + 1))
                            act.copy(O[:, k % 2], OB[k % 2][:, :, 0:DV]).then_inc(act_o, 1)
                        prepared += prepares

                @block.vector
                def _(dve):
                    v = Chain(dve, dve_s)
                    prepared = 0
                    for k, (runs, prepares) in enumerate(steps):
                        a, par, now = prepared, (odd + k + 1) % 2, (odd + k) % 2

                        def rotate_k(i):
                            t = slice(128 * i, 128 * i + 128)
                            if i == 0:
                                dve.wait_ge(l_tab, 32 * (a + 1))
                                dve.wait_ge(act_t, 4 * a + 2)
                                if runs and k:
                                    dve.wait_ge(pe_o, NC * k)
                            if NT * a + i:
                                dve.wait_ge(rot_k, NT * a + i)
                            v(dve.tensor_tensor(KQ[:, par, :, t], cosF[:, :, t], bcast(kqT[:, 0, t], 1, PAIRS), ALU.mult))
                            v.link(dve.tensor_tensor(tmpv[:, :, :], sinF[:, :, t], bcast(kqT[:, 1, t], 1, PAIRS), ALU.mult))
                            dve.tensor_tensor(KQ[:, par, :, t], KQ[:, par, :, t], tmpv[:, :, :], ALU.add).then_inc(rot_k, 1)

                        def take_scores(i):
                            dve.wait_ge(pe_s, NT * a + i + 1)
                            if i == 0:
                                dve.wait_ge(d_exp, a + 1)
                                if a:
                                    dve.wait_ge(xt_done, a)
                            chunks = slice(4 * i, 4 * i + 4)
                            scores = prep[i % 2][:, :].rearrange("p (s c z i) -> p s c z i", s=SIDES, c=4, z=2)
                            v(dve.tensor_tensor(AT[:, :, chunks, :], scores[:, :, :, 0, :], DB[:, :, chunks, :], ALU.mult))
                            for s in range(SIDES):
                                last = dve.scalar_tensor_tensor(
                                    out=PT[:, par, s, chunks, :], in0=scores[:, s, :, 1, :], scalar=wq[par][:, s:s + 1],
                                    in1=DB[:, s, chunks, :], op0=ALU.mult, op1=ALU.mult)
                                last.then_inc(scored, 1)

                        def to_lanes():
                            v.wait()
                            v(dve.transpose(AL[:, :, :], AT[:, :, :, :].rearrange("p s c i -> p i (s c)")))
                            v.link(dve.tensor_copy(XL[:, :, :].rearrange("p i j -> p (i j)"), eye[:, :]))

                        def eliminate(r):
                            rows, done = C - 1 - r, r + 1
                            e = EL[:, 0:rows * done].rearrange("p (i j) -> p i j", i=rows)
                            v.link(dve.tensor_tensor(e, bcast(AL[:, r + 1:, r], 2, done), bcast(XL[:, r, 0:done], 1, rows), ALU.mult))
                            v.link(dve.tensor_tensor(XL[:, r + 1:, 0:done], XL[:, r + 1:, 0:done], e, ALU.subtract))

                        def from_lanes():
                            dve.transpose(XT[:, par].rearrange("p s c i -> p i (s c)"), XL[:, :, :]).then_inc(xt_done, 1)
                            dve.wait_ge(xt_done, a + 1)

                        def scale_q(p):
                            if p == 0:
                                dve.wait_ge(l_eg, 32 * (a + 1))
                                dve.wait_ge(rot_q, NT * (a + 1))
                            last = dve.scalar_tensor_tensor(out=Qd[:, par, p], in0=EG[:, p], scalar=wp[par][:, p:p + 1],
                                                            in1=KQ[:, 2, p], op0=ALU.mult, op1=ALU.mult)
                            if p < PAIRS - 1:
                                v(last)
                            else:
                                last.then_inc(qd_done, 1)

                        def keep_decay():
                            dve.wait_ge(l_eg, 32 * (a + 1))
                            dve.tensor_copy(decay[:, par], EG[:, :, C - 1::C]).then_inc(qd_done, 1)

                        def weights():
                            h = (n0 + (k + 1)) // B
                            v(dve.tensor_copy(wq[par][:, :], w_side[:, bass.ds(h, 1), :].rearrange("p a s -> p (a s)")))
                            v.link(dve.tensor_copy(wp[par][:, :], w_pair[:, bass.ds(h, 1), :].rearrange("p a s -> p (a s)")))

                        jobs = []
                        if prepares:
                            jobs += [weights]
                            jobs += [lambda i=i: rotate_k(i) for i in range(NT)]
                            jobs += [lambda i=i: take_scores(i) for i in range(NT)]
                            jobs += [to_lanes] + [lambda r=r: eliminate(r) for r in range(C - 1)] + [from_lanes]
                            jobs += [keep_decay] + [lambda p=p: scale_q(p) for p in range(PAIRS)]
                        if not runs:
                            for job in jobs:
                                job()
                        else:
                            places = DVE_PLACES if prepares else [0] * (2 * NC)
                            for c in range(NC):
                                for s in range(SIDES):
                                    if c:
                                        dve.wait_ge(pe_r[s], (NC - 1) * k + c)
                                        dve.scalar_tensor_tensor(
                                            out=R[:, s, :], in0=RW[s][:, 0:DV], scalar=col[:, now, 1, s, c:c + 1],
                                            in1=KV[:, now, c, DK:], op0=ALU.mult, op1=ALU.add).then_inc(dve_r[s], 1)
                                for _ in range(places[2 * c]):
                                    jobs.pop(0)()
                                if c < NC - 1:
                                    for s in range(SIDES):
                                        dve.wait_ge(pe_f[s], (NC - 1) * k + c + 1)
                                        if c:
                                            dve.wait_ge(dve_f[s], 2 * ((NC - 1) * k + c))
                                        for p, new in ((2 * s, RW[s][:, 2 * DV:3 * DV]), (2 * s + 1, SB[s][:, 0:DV])):
                                            if c == 0:
                                                last = dve.tensor_copy(S[:, (c + 1) % 2, p, :], new)
                                            else:
                                                last = dve.scalar_tensor_tensor(
                                                    out=S[:, (c + 1) % 2, p, :], in0=S[:, c % 2, p, :],
                                                    scalar=decay[:, now, p, c:c + 1], in1=new, op0=ALU.mult, op1=ALU.add)
                                            last.then_inc(dve_f[s], 1)
                                for _ in range(places[2 * c + 1]):
                                    jobs.pop(0)()
                            assert not jobs, len(jobs)
                        prepared += prepares

                @block.tensor
                def _(pe):
                    prepared = 0
                    for k, (runs, prepares) in enumerate(steps):
                        a, par, now = prepared, (odd + k + 1) % 2, (odd + k) % 2

                        def transposes(r):
                            if r == 0:
                                pe.wait_ge(l_win, 16 * (a + 1))
                            if r < 2:
                                if a:
                                    pe.wait_ge(scored, 2 * (NT * (a - 1) + 3 + r))
                            else:
                                pe.wait_ge(act_t, 4 * a + r - 1)
                            off = WIN * (r // 2) + HALF * (r % 2)
                            for i in range(NT):
                                last = pe.transpose(prep[r % 2][:, 128 * i:128 * i + 128], win[:, i, off:off + 128], ident[:, :])
                            last.then_inc(pe_t, 1)

                        def scores(i, c4):
                            if c4 == 0:
                                pe.wait_ge(rot_k, NT * a + i + 1)
                                pe.wait_ge(rot_q, NT * a + i + 1)
                                if i < 2:
                                    pe.wait_ge(act_t, 4 * a + 3 + i)
                                else:
                                    pe.wait_ge(scored, 2 * (NT * a + i - 1))
                            c = 4 * i + c4
                            t = slice(C * c, C * c + C)
                            for s in range(SIDES):
                                for q in range(QUADS):
                                    p, e = pair_of(s, q), q % 2
                                    rows = slice(64 * e, 64 * e + 64)
                                    at = 256 * s + 64 * c4
                                    last = pe.matmul(prep[i % 2][32 * q:32 * q + 32, at:at + 64], KQ[rows, par, p, t],
                                                     KQ[rows, par::2 - par, p, t], start=True, stop=True)
                            if c4 == 3:
                                last.then_inc(pe_s, 1)

                        def read_state(s, c):
                            pe.wait_ge(dve_f[s], 2 * ((NC - 1) * k + c))
                            for q in range(QUADS):
                                p, e = pair_of(s, q), q % 2
                                rows = slice(64 * e, 64 * e + 64)
                                last = pe.matmul(RW[s][32 * q:32 * q + 32, 0:DV], KQ[rows, now, p, C * c:C * c + C],
                                                 S[rows, c % 2, p, :], start=True, stop=True)
                            last.then_inc(pe_r[s], 1)

                        def solve(s, c):
                            if c:
                                pe.wait_ge(dve_r[s], (NC - 1) * k + c)
                            elif k:
                                pe.wait_ge(act_w[s], NC * k)
                            for q in range(QUADS):
                                rows = slice(32 * q, 32 * q + 32)
                                rhs = R[rows, s, :] if c else KV[rows, now, c, DK:]
                                last = pe.matmul(RW[s][rows, DV:2 * DV], XT[rows, now, s, c, :], rhs, start=True, stop=True)
                            last.then_inc(pe_w[s], 1)

                        def write_state(s, c):
                            pe.wait_ge(act_w[s], NC * k + c + 1)
                            for q in range(QUADS):
                                e = q % 2
                                rows = slice(32 * q, 32 * q + 32)
                                to = RW[s][64 * e:64 * e + 64, 2 * DV:3 * DV] if q < 2 else SB[s][64 * e:64 * e + 64, 0:DV]
                                last = pe.matmul(to, KD[rows, now, s, c, :], W[rows, s, :], start=True, stop=True)
                            last.then_inc(pe_f[s], 1)

                        def output(c):
                            to = OB[now][32 * (c % 4):32 * (c % 4) + 32, c // 4, 0:DV]
                            if c == NC - 1:
                                for s in range(SIDES):
                                    pe.wait_ge(act_w[s], NC * k + c + 1)
                            for s in range(SIDES):
                                last = pe.matmul(to, PT[:, now, s, c, :], W[:, s, :], start=(s == 0), stop=(s == 1 and c == 0))
                            if c:
                                for p in range(PAIRS):
                                    last = pe.matmul(to, Qd[:, now, p, C * c:C * c + C], S[:, c % 2, p, :],
                                                     start=False, stop=(p == PAIRS - 1))
                            last.then_inc(pe_o, 1)

                        jobs = []
                        if prepares:
                            jobs += [lambda r=r: transposes(r) for r in range(4)]
                            jobs += [lambda i=i, c4=c4: scores(i, c4) for i in range(NT) for c4 in range(4)]
                        if not runs:
                            for job in jobs:
                                job()
                        else:
                            places = PE_PLACES if prepares else [0] * (2 * NC)
                            for c in range(NC):
                                for s in range(SIDES):
                                    if c:
                                        read_state(s, c)
                                for _ in range(places[2 * c]):
                                    jobs.pop(0)()
                                for s in range(SIDES):
                                    solve(s, c)
                                for _ in range(places[2 * c + 1]):
                                    jobs.pop(0)()
                                if c < NC - 1:
                                    for s in range(SIDES):
                                        write_state(s, c)
                                output(c)
                            assert not jobs, len(jobs)
                        if prepares and k + 1 < len(steps):
                            pe.wait_ge(xt_done, a + 1)
                            pe.wait_ge(kd_done, a + 1)
                            pe.wait_ge(qd_done, 2 * (a + 1))
                            pe.wait_ge(scored, 2 * NT * (a + 1))
                        prepared += prepares
            fresh()

        wq = [sb(f"wq_{p}", [128, SIDES]) for p in range(2)]
        wp = [sb(f"wp_{p}", [128, PAIRS]) for p in range(2)]
        POOL_GR, POOL_STEP = 1, 1 + 2 * NT + 2 * (4 + 2) + 1
        PE_PLACES = [0] * (2 * NC)
        for c, m in ((0, 2), (1, 2)):
            PE_PLACES[2 * c + 1] = m
        for c in range(4, 8):
            PE_PLACES[2 * c], PE_PLACES[2 * c + 1] = 2, 2
        DVE_PLACES = [0] * (2 * NC)
        for c, m in ((1, 2), (2, 1), (3, 1), (4, 1), (5, 1), (6, 1), (7, 1), (8, 2)):
            DVE_PLACES[2 * c] = m
        rest = (C - 1) + 1 + 1 + PAIRS
        late = 2 * NC - 17
        for i in range(late):
            DVE_PLACES[17 + i] = (i + 1) * rest // late - i * rest // late

        emit(-1, 1, [(False, True)])
        with nc.Fori(0, NSEQ // 2 - 1) as r:
            emit(r * 2, 0, [(True, True), (True, True)])
        emit(NSEQ - 2, 0, [(True, True), (True, False)])


def experts(nc, sems, fresh, x, Wg, Wo, gate_w, w13, w2, c_small, ident, xnT, O_s, out):
    KT = H * DV // 128
    IC = 2 * INTER // 128
    with ExitStack() as ctx:
        def sb(name, shape):
            return ctx.enter_context(nc.sbuf_tensor("moe_" + name, shape, F32))

        def ps(name, shape):
            return ctx.enter_context(nc.psum_tensor("moe_" + name, shape, F32))

        wg, wo = sb("wg", [128, H * DV]), sb("wo", [128, KT, D])
        gw, gwT = sb("gw", [E_X, D]), sb("gwT", [D, E_X])
        w13T = sb("w13T", [D, E_X, IC, 128])
        w2T = sb("w2T", [128, E_X, INTER // 128, D])
        earlier = sb("earlier", [128, E_X, E_X])
        earlier_g = sb("earlier_g", [128, GROUPS, GROUPS])
        bank = [ps(f"ebank{i}", [128, 512]) for i in range(8)]
        sm = sems
        with ExitStack() as part:
            nat13 = part.enter_context(nc.sbuf_tensor("nat13", [128, E_X, IC, D], F32))
            nat2 = part.enter_context(nc.sbuf_tensor("nat2", [D, E_X, INTER], F32))
            loaded, turned, copied = sm[:3]
            with nc.Block() as block:
                @block.sync
                def _(sp):
                    sp.dma_start(wg[:, :], Wg).then_inc(loaded, 16)
                    sp.dma_start(wo[:, :, :], Wo.rearrange("(k p) n -> p k n", p=128)).then_inc(loaded, 16)
                    sp.dma_start(gw[:, :], gate_w).then_inc(loaded, 16)
                    sp.dma_start(nat13[:, :, :, :], w13.rearrange("e (i p) d -> p e i d", p=128)).then_inc(loaded, 16)
                    sp.dma_start(nat2[:, :, :], w2.rearrange("e d i -> d e i")).then_inc(loaded, 16)
                    sp.dma_start(earlier[:, :, :].rearrange("p a b -> p (a b)"),
                                 c_small[1:2, 0:64].broadcast_to([128, 64])).then_inc(loaded, 16)
                    sp.dma_start(earlier_g[:, :, :].rearrange("p a b -> p (a b)"),
                                 c_small[1:2, 64:80].broadcast_to([128, 16])).then_inc(loaded, 16)
                    sp.wait_ge(loaded, 7 * 16)

                @block.tensor
                def _(pe):
                    pe.wait_ge(loaded, 7 * 16)
                    pe.transpose(bank[0][:, 0:E_X], gw[:, :], ident[0:E_X, 0:E_X]).then_inc(turned, 1)
                    for e in range(E_X):
                        if e:
                            pe.wait_ge(copied, 1 + 2 * e)
                        for i in range(IC):
                            last = pe.transpose(bank[1][:, 128 * i:128 * i + 128], nat13[:, e, i, :], ident[:, :])
                        last.then_inc(turned, 1)
                        for i in range(INTER // 128):
                            last = pe.transpose(bank[2][:, 128 * i:128 * i + 128], nat2[:, e, 128 * i:128 * i + 128], ident[:, :])
                        last.then_inc(turned, 1)

                @block.vector
                def _(dve):
                    dve.wait_ge(turned, 1)
                    dve.tensor_copy(gwT[:, :], bank[0][:, 0:E_X]).then_inc(copied, 1)
                    for e in range(E_X):
                        dve.wait_ge(turned, 2 + 2 * e)
                        dve.tensor_copy(w13T[:, e, :, :].rearrange("p i k -> p (i k)"), bank[1][:, :]).then_inc(copied, 1)
                        dve.wait_ge(turned, 3 + 2 * e)
                        dve.tensor_copy(w2T[:, e, :, :].rearrange("p i k -> p (i k)"), bank[2][:, 0:INTER]).then_inc(copied, 1)
            fresh()

        o = sb("o", [128, NT, H * DV])
        gate = sb("gate", [128, NT, H * DV])
        xs = sb("exs", [128, NT, D])
        xT = sb("exT", [128, T])
        oT = sb("oT", [128, KT, T])
        x1 = sb("x1", [128, NT, D])
        xn = sb("exn", [128, NT, D])
        sq = sb("esq", [128, NT, D])
        stat, std = sb("estat", [128, NT]), sb("estd", [128, NT])
        x2T = sb("x2T", [D, T])
        sc = sb("sc", [128, NT, E_X])
        red = sb("red", [128, NT])
        grp = sb("grp", [128, NT, GROUPS])
        cg, cg2 = sb("cg", [128, NT, GROUPS, GROUPS]), sb("cg2", [128, NT, GROUPS, GROUPS])
        ce, ce2 = sb("ce", [128, NT, E_X, E_X]), sb("ce2", [128, NT, E_X, E_X])
        rank_g, rank = sb("rank_g", [128, NT, GROUPS]), sb("rank", [128, NT, E_X])
        comb = sb("comb", [128, NT, E_X])
        sil = sb("sil", [128, 2, T])
        hid = sb("hid", [128, 2, 2, T])
        acc = sb("acc", [128, NT, D])
        (l_x, l_o, xt_in, pe_g, sig, gated, pe_to, oT_s, pe_y, dve_s, std_in, std_out, xn_in, pe_x2, x2_s, pe_sc,
         e_in, e_out, pe_h, act_h, dve_h, pe_z, dve_z, stored, gate_f) = sm[:25]
        with nc.Fori(0, B) as b:
            with nc.Block() as block:
                @block.sync
                def _(sp):
                    sp.dma_start(xs[:, :, :], x[bass.ds(b, 1)].rearrange("a (i p) d -> p (a i) d", p=128)).then_inc(l_x, 16)
                    for i in range(NT):
                        sp.dma_start(o[:, i, :].rearrange("p (h v) -> p h v", h=H),
                                     O_s.rearrange("(h b) (i p) v -> h b i p v", b=B, p=128)[:, bass.ds(b, 1), i].rearrange("h a p v -> p (h a) v")).then_inc(l_o, 16)
                    sp.wait_ge(dve_z, E_X * NT)
                    sp.dma_start(out[bass.ds(b, 1)].rearrange("a (i p) d -> p (a i) d", p=128), acc[:, :, :]).then_inc(stored, 16)
                    sp.wait_ge(stored, 16)

                @block.gpsimd
                def _(pool):
                    pool.tensor_copy(xT[:, :], xnT[:, bass.ds(b * T, T)]).then_inc(xt_in, 1)

                @block.tensor
                def _(pe):
                    pe.wait_ge(xt_in, 1)
                    for i in range(NT):
                        pe.matmul(bank[i][:, :], xT[:, 128 * i:128 * i + 128], wg[:, :], start=True, stop=True).then_inc(pe_g, 1)
                    for k in range(KT):
                        for i in range(NT):
                            pe.wait_ge(gated, i + 1)
                            last = pe.transpose(bank[4 + k][:, 128 * i:128 * i + 128], o[:, i, 128 * k:128 * k + 128], ident[:, :])
                        last.then_inc(pe_to, 1)
                    pe.wait_ge(oT_s, KT)
                    for i in range(NT):
                        for k in range(KT):
                            last = pe.matmul(bank[0][:, D * i:D * i + D], oT[:, k, 128 * i:128 * i + 128], wo[:, k, :],
                                             start=(k == 0), stop=(k == KT - 1))
                    last.then_inc(pe_y, 1)
                    pe.wait_ge(xn_in, 1)
                    for i in range(NT):
                        last = pe.transpose(bank[1][:, 128 * i:128 * i + 128], xn[:, i, :], ident[:, :])
                    last.then_inc(pe_x2, 1)
                    pe.wait_ge(x2_s, 1)
                    for i in range(NT):
                        last = pe.matmul(bank[2][:, E_X * i:E_X * i + E_X], x2T[:, 128 * i:128 * i + 128], gwT[:, :], start=True, stop=True)
                    last.then_inc(pe_sc, 1)

                    def up(e):
                        for j in range(2):
                            if e == 0 and j == 0:
                                pe.wait_ge(e_in, 1)
                            if e:
                                pe.wait_ge(dve_h, 2 * (e - 1) + j + 1)
                            pe.matmul(bank[2 + 2 * j][:, :], w13T[:, e, j, :], x2T[:, :], start=True, stop=True)
                            pe.matmul(bank[3 + 2 * j][:, :], w13T[:, e, 2 + j, :], x2T[:, :], start=True, stop=True).then_inc(pe_h, 1)

                    def down(e):
                        pe.wait_ge(dve_h, 2 * e + 2)
                        if e >= 2:
                            pe.wait_ge(dve_z, NT * (e - 1))
                        for i in range(NT):
                            for j in range(2):
                                last = pe.matmul(bank[6 + e % 2][:, D * i:D * i + D], hid[:, e % 2, j, 128 * i:128 * i + 128],
                                                 w2T[:, e, j, :], start=(j == 0), stop=(j == 1))
                        last.then_inc(pe_z, 1)

                    up(0)
                    for e in range(E_X):
                        if e + 1 < E_X:
                            up(e + 1)
                        down(e)

                @block.scalar
                def _(act):
                    for i in range(NT):
                        act.wait_ge(pe_g, i + 1)
                        act.activation(gate[:, i, :], bank[i][:, :], ACT.Sigmoid).then_inc(sig, 1)
                    for k in range(KT):
                        act.wait_ge(pe_to, k + 1)
                        act.copy(oT[:, k, :], bank[4 + k][:, :]).then_inc(oT_s, 1)
                    act.wait_ge(std_in, 1)
                    act.activation(std[:, :], std[:, :], ACT.Sqrt).then_inc(std_out, 1)
                    act.wait_ge(pe_x2, 1)
                    act.copy(x2T[:, :], bank[1][:, :]).then_inc(x2_s, 1)
                    act.wait_ge(e_in, 1)
                    act.activation(sc[:, :, :], sc[:, :, :], ACT.Exp).then_inc(e_out, 1)
                    for e in range(E_X):
                        for j in range(2):
                            act.wait_ge(pe_h, 2 * e + j + 1)
                            if e:
                                act.wait_ge(dve_h, 2 * (e - 1) + j + 1)
                            act.activation(sil[:, j, :], bank[2 + 2 * j][:, :], ACT.Silu).then_inc(act_h, 1)

                @block.vector
                def _(dve):
                    v = Chain(dve, dve_s)
                    for i in range(NT):
                        dve.wait_ge(sig, i + 1)
                        dve.wait_ge(l_o, 16 * NT)
                        dve.tensor_tensor(o[:, i, :], o[:, i, :], gate[:, i, :], ALU.mult).then_inc(gated, 1)
                    dve.wait_ge(pe_y, 1)
                    dve.wait_ge(l_x, 16)
                    x1v = x1[:, :, :].rearrange("p i d -> p (i d)")
                    v.link(dve.tensor_tensor(x1v, xs[:, :, :].rearrange("p i d -> p (i d)"), bank[0][:, :], ALU.add))
                    v.link(dve.tensor_reduce(stat[:, :], x1[:, :, :], AX_X, ALU.add))
                    v.link(dve.tensor_scalar(stat[:, :], stat[:, :], 1.0 / D, None, ALU.mult))
                    v.link(dve.tensor_tensor(xn[:, :, :], x1[:, :, :], bcast(stat[:, :], 2, D), ALU.subtract))
                    v.link(dve.tensor_tensor(sq[:, :, :], xn[:, :, :], xn[:, :, :], ALU.mult))
                    v.link(dve.tensor_reduce(stat[:, :], sq[:, :, :], AX_X, ALU.add))
                    dve.tensor_scalar(std[:, :], stat[:, :], 1.0 / D, 1e-5, ALU.mult, ALU.add).then_inc(std_in, 1)
                    dve.wait_ge(std_out, 1)
                    v.link(dve.reciprocal(std[:, :], std[:, :]))
                    dve.tensor_tensor(xn[:, :, :], xn[:, :, :], bcast(std[:, :], 2, D), ALU.mult).then_inc(xn_in, 1)
                    dve.wait_ge(pe_sc, 1)
                    raw = bank[2][:, 0:NT * E_X].rearrange("p (i e) -> p i e", i=NT)
                    v.link(dve.tensor_reduce(red[:, :], raw, AX_X, ALU.max))
                    dve.tensor_tensor(sc[:, :, :], raw, bcast(red[:, :], 2, E_X), ALU.subtract).then_inc(e_in, 1)
                    dve.wait_ge(e_out, 1)
                    v.link(dve.tensor_reduce(red[:, :], sc[:, :, :], AX_X, ALU.add))
                    v.link(dve.reciprocal(red[:, :], red[:, :]))
                    v.link(dve.tensor_tensor(sc[:, :, :], sc[:, :, :], bcast(red[:, :], 2, E_X), ALU.mult))
                    per = E_X // GROUPS
                    v.link(dve.tensor_tensor(grp[:, :, :], sc[:, :, 0::per], sc[:, :, 1::per], ALU.max))

                    def ranks(values, n, to, one, two, first_wins):
                        for i in range(NT):
                            other = bcast(values[:, i, :], 1, n)
                            own = bcast(values[:, i, :], 2, n)
                            v(dve.tensor_tensor(one[:, i], other, own, ALU.is_equal))
                            v(dve.tensor_tensor(two[:, i], other, own, ALU.is_gt))
                        v.wait()
                        for i in range(NT):
                            v(dve.tensor_tensor(one[:, i], one[:, i], first_wins[:, :, :], ALU.mult))
                        v.wait()
                        v.link(dve.tensor_tensor(one[:, :, :, :], one[:, :, :, :], two[:, :, :, :], ALU.add))
                        v.link(dve.tensor_reduce(to[:, :, :], one[:, :, :, :], AX_X, ALU.add))

                    ranks(grp, GROUPS, rank_g, cg, cg2, earlier_g)
                    v.link(dve.tensor_scalar(rank_g[:, :, :], rank_g[:, :, :], 2.0, None, ALU.is_lt))
                    for j in range(per):
                        v(dve.tensor_tensor(sc[:, :, j::per], sc[:, :, j::per], rank_g[:, :, :], ALU.mult))
                    v.wait()
                    ranks(sc, E_X, rank, ce, ce2, earlier)
                    v.link(dve.tensor_scalar(rank[:, :, :], rank[:, :, :], 2.0, None, ALU.is_lt))
                    v.link(dve.tensor_tensor(comb[:, :, :], sc[:, :, :], rank[:, :, :], ALU.mult))
                    v.link(dve.tensor_reduce(red[:, :], comb[:, :, :], AX_X, ALU.add))
                    v.link(dve.reciprocal(red[:, :], red[:, :]))
                    v.link(dve.tensor_tensor(comb[:, :, :], comb[:, :, :], bcast(red[:, :], 2, E_X), ALU.mult))

                    def hidden(e):
                        for j in range(2):
                            dve.wait_ge(act_h, 2 * e + j + 1)
                            if e >= 2:
                                dve.wait_ge(pe_z, e - 1)
                            dve.tensor_tensor(hid[:, e % 2, j, :], sil[:, j, :], bank[3 + 2 * j][:, :], ALU.mult).then_inc(dve_h, 1)

                    def add(e):
                        dve.wait_ge(pe_z, e + 1)
                        if e:
                            dve.wait_ge(dve_z, NT * e)
                        for i in range(NT):
                            dve.scalar_tensor_tensor(out=acc[:, i, :], in0=bank[6 + e % 2][:, D * i:D * i + D],
                                                     scalar=comb[:, i, e:e + 1], in1=acc[:, i, :] if e else x1[:, i, :],
                                                     op0=ALU.mult, op1=ALU.add).then_inc(dve_z, 1)

                    hidden(0)
                    for e in range(E_X):
                        if e + 1 < E_X:
                            hidden(e + 1)
                        add(e)
            fresh()


_INS = ["L0_attn_hidden_states", "L0_attn_Wq", "L0_attn_Wk", "L0_attn_Wv", "L0_attn_Wbeta", "L0_attn_Wtg",
        "L0_attn_mode_logits", "L0_attn_log_decay", "L0_attn_omega_log_scale", "L0_attn_Wg", "L0_attn_Wo",
        "L0_ffn_gate_w", "L0_ffn_w13_weight", "L0_ffn_w2_weight"]


def _constants(np):
    f = np.float32
    at = np.arange(128)
    same = (at[:, None] // C) == (at[None, :] // C)
    mat = np.zeros((4, 128, 128), f)
    mat[0] = np.eye(128)
    mat[1] = same & (at[:, None] <= at[None, :])
    mat[2] = same
    mat[3, :, 0:C] = np.where((at % C)[:, None] <= np.arange(C)[None, :], 0.0, -1e30)
    freq = (f(1.0) / f(10000.0) ** (np.arange(0, DK, 2, dtype=f) / f(DK))).astype(f)
    pos = np.zeros((128, T + NC + HALF), f)
    pos[:, 0:T] = np.arange(T)
    pos[:, T:T + NC] = (at % C)[:, None] + C * np.arange(NC)[None, :]
    pos[:, T + NC:] = freq
    col = np.zeros((128, 4), f)
    col[:, 0] = freq[at % HALF]
    col[:, 1] = np.where(at % DK < HALF, 1.0, -1.0)
    col[:, 2] = f(np.pi / 2)
    small = np.zeros((2, C * C), f)
    small[0] = np.eye(C).reshape(-1)
    small[1, 0:64] = (np.arange(E_X)[None, :] < np.arange(E_X)[:, None]).reshape(-1)
    small[1, 64:80] = (np.arange(GROUPS)[None, :] < np.arange(GROUPS)[:, None]).reshape(-1)
    return {"c_mat": mat, "c_pos": pos, "c_col": col, "c_small": small}


def kernel(**inputs):
    import numpy as _np
    import concourse.bacc as _bacc
    from concourse.bass_utils import run_bass_kernel_spmd as _run

    nc = _bacc.Bacc("TRN2", target_bir_lowering=False, num_devices=1)
    arrays, args = {}, []
    given = {name: _np.ascontiguousarray(inputs[name]) for name in _INS}
    for name, a in {**given, **_constants(_np)}.items():
        arrays[f"in_{name}_dram"] = a
        args.append(nc.dram_tensor(f"in_{name}_dram", a.shape, mybir.dt.from_np(a.dtype), kind="ExternalInput").ap())
    out = nc.dram_tensor("out_0_dram", (B, T, D), F32, kind="ExternalOutput").ap()
    program(nc, *args, out)
    r = _run(nc, [arrays], core_ids=[0])
    return r.results[0]["out_0_dram"]
```

```python
from contextlib import ExitStack

import concourse.bass as bass
from concourse import mybir

F32 = mybir.dt.float32
ALU = mybir.AluOpType
ACT = mybir.ActivationFunctionType
AX_X = mybir.AxisListType.X

B, T, D = 8, 512, 128
H, DK, DV, M = 8, 64, 64, 8
HALF = DK // 2
C = 32
NC = T // C
NSEQ = H * B
NT = T // 128
PAIRS = M // 2
SIDES = 2
QUADS = 4
UNITS = SIDES * NC
HM = H * M
E_X, GROUPS, INTER = 8, 4, 256
WIN = DK * 3 // 2
TWO_PI = 6.283185307179586
PI = 3.1415925
CW1 = 6.28125
CW2 = 0.0019350051879882812
CW3 = TWO_PI - CW1 - CW2
ROUND = 12582912.0
CLAMP = 44.0


class Chain:

    def __init__(self, eng, sem):
        self.eng, self.sem, self.n, self.seen = eng, sem, 0, 0

    def __call__(self, ins):
        ins.then_inc(self.sem, 1)
        self.n += 1
        return self.n

    def wait(self, n=None):
        n = self.n if n is None else n
        if n > self.seen:
            self.eng.wait_ge(self.sem, n)
            self.seen = n

    def link(self, ins):
        self(ins)
        self.wait()


POOL_Q, DVE_SIN = 3, 2


def bcast(ap, axis, n):
    ap = ap.unsqueeze(axis)
    return ap.broadcast_to([*ap.shape[:axis], n, *ap.shape[axis + 1:]])


def program(nc, x, Wq, Wk, Wv, Wbeta, Wtg, mode_logits, log_decay, omega_log, Wg, Wo, gate_w, w13, w2,
            c_mat, c_pos, c_col, c_small, out):
    def dram(name, shape):
        return nc.dram_tensor(name, shape, F32, kind="Internal").ap()

    KQ_s = dram("KQ_s", (H, B, 128, NT, 2 * WIN))
    KV_s = dram("KV_s", (H, B, C, NC, 2 * DK))
    G_s = dram("G_s", (H, B, M, T))
    EG_s = dram("EG_s", (H, B, M, T))
    COL_s = dram("COL_s", (H, B, 128, 3, SIDES, NC))
    COSF_s = dram("COSF_s", (H, 2, HALF, PAIRS, T))
    SINF_s = dram("SINF_s", (H, 2, HALF, PAIRS, T))
    COST_s = dram("COST_s", (H, 128, SIDES, NC, HALF))
    SINT_s = dram("SINT_s", (H, 128, SIDES, NC, HALF))
    O_s = dram("O_s", (NSEQ, T, DV))
    XN_s = dram("XN_s", (B, D, T))

    with ExitStack() as whole:
        def keep(name, shape):
            return whole.enter_context(nc.sbuf_tensor(name, shape, F32))

        sems = [nc.alloc_semaphore(f"phase_{i}") for i in range(44)]
        first = sems[0].num
        assert [s.num for s in sems] == list(range(first, first + 44))

        def fresh():
            nc.all_engine_barrier(sems_to_clear=range(first, first + 44))

        ident = keep("ident", [128, 128])
        w_side = keep("w_side", [128, H, SIDES])
        w_pair = keep("w_pair", [128, H, PAIRS])

        prepare(nc, sems, fresh, x, Wq, Wk, Wv, Wbeta, Wtg, mode_logits, log_decay, omega_log,
                c_mat, c_pos, c_col, ident, XN_s, w_side, w_pair,
                KQ_s, KV_s, G_s, EG_s, COL_s, COSF_s, SINF_s, COST_s, SINT_s)
        recurrence(nc, sems, fresh, c_mat, c_small, ident, w_side, w_pair,
                   KQ_s, KV_s, G_s, EG_s, COL_s, COSF_s, SINF_s, COST_s, SINT_s, O_s)
        experts(nc, sems, fresh, x, Wg, Wo, gate_w, w13, w2, c_small, ident, XN_s, O_s, out)


def prepare(nc, sems, fresh, x, Wq, Wk, Wv, Wbeta, Wtg, mode_logits, log_decay, omega_log,
            c_mat, c_pos, c_col, ident, XN_s, w_side, w_pair,
            KQ_s, KV_s, G_s, EG_s, COL_s, COSF_s, SINF_s, COST_s, SINT_s):
    with ExitStack() as ctx:
        def sb(name, shape):
            return ctx.enter_context(nc.sbuf_tensor("set_" + name, shape, F32))

        tri, ones_c = sb("tri", [128, 128]), sb("ones_c", [128, 128])
        wq, wk, wv = sb("wq", [128, H * DK]), sb("wk", [128, H * DK]), sb("wv", [128, H * DV])
        wbt = sb("wbt", [128, 2 * HM])
        rho, modes, om = sb("rho", [128, HM]), sb("modes", [128, H, M]), sb("om", [128, H, M])
        mx = sb("mx", [128, H])
        om_side = sb("om_side", [128, H, SIDES])
        raw = sb("raw", [128, 3, B * NT, HM])
        loaded, dve_s = sems[0], sems[1]
        exp_in, exp_out, put = sems[2], sems[3], sems[4]

        with nc.Block() as block:
            @block.sync
            def _(sp):
                sp.dma_start(ident[:, :], c_mat[0]).then_inc(loaded, 16)
                sp.dma_start(tri[:, :], c_mat[1]).then_inc(loaded, 16)
                sp.dma_start(ones_c[:, :], c_mat[2]).then_inc(loaded, 16)
                sp.dma_start(rho[:, :], log_decay.rearrange("(a h) m -> a (h m)", a=1).broadcast_to([128, HM])).then_inc(loaded, 16)
                sp.dma_start(modes[:, :, :], bcast(mode_logits, 0, 128)).then_inc(loaded, 16)
                sp.dma_start(om[:, :, :], bcast(omega_log, 0, 128)).then_inc(loaded, 16)
                sp.dma_start(wbt[:, 0:HM], Wbeta).then_inc(loaded, 16)
                sp.dma_start(wbt[:, HM:], Wtg).then_inc(loaded, 16)
                sp.dma_start(wq[:, :], Wq).then_inc(loaded, 16)
                sp.dma_start(wk[:, :], Wk).then_inc(loaded, 16)
                sp.dma_start(wv[:, :], Wv).then_inc(loaded, 16)
                sp.wait_ge(loaded, 11 * 16)

            @block.scalar
            def _(act):
                act.wait_ge(loaded, 11 * 16)
                act.activation(rho[:, :], rho[:, :], ACT.Exp).then_inc(exp_out, 1)
                act.activation(om[:, :, :], om[:, :, :], ACT.Exp).then_inc(exp_out, 1)
                act.wait_ge(exp_in, 1)
                act.activation(modes[:, :, :], modes[:, :, :], ACT.Exp).then_inc(exp_out, 1)

            @block.vector
            def _(dve):
                v = Chain(dve, dve_s)
                dve.wait_ge(loaded, 11 * 16)
                v.link(dve.tensor_reduce(mx[:, :], modes[:, :, :], AX_X, ALU.max))
                dve.tensor_tensor(modes[:, :, :], modes[:, :, :], bcast(mx[:, :], 2, M), ALU.subtract).then_inc(exp_in, 1)
                dve.wait_ge(exp_out, 3)
                v.link(dve.tensor_reduce(mx[:, :], modes[:, :, :], AX_X, ALU.add))
                v.link(dve.reciprocal(mx[:, :], mx[:, :]))
                v.link(dve.tensor_tensor(modes[:, :, :], modes[:, :, :], bcast(mx[:, :], 2, M), ALU.mult))
                v.link(dve.tensor_scalar(rho[:, :], rho[:, :], 1.0, None, ALU.add))
                v.link(dve.reciprocal(rho[:, :], rho[:, :]))
                for q in range(QUADS):
                    rows = slice(32 * q, 32 * q + 32)
                    v(dve.tensor_copy(w_side[rows, :, :], modes[rows, :, q::QUADS]))
                    v(dve.tensor_copy(om_side[rows, :, :], om[rows, :, q::QUADS]))
                for e in range(2):
                    rows = slice(64 * e, 64 * e + 64)
                    v(dve.tensor_copy(w_pair[rows, :, :], modes[rows, :, e::2]))
                v.wait()
        fresh()

        project(nc, sems, fresh, x, wq, wk, wv, wbt, rho, tri, ones_c, ident, XN_s, raw, KQ_s, KV_s, G_s, EG_s)

        with ExitStack() as part:
            cols = part.enter_context(nc.sbuf_tensor("cols", [128, NSEQ, 3, SIDES, NC], F32))
            with nc.Block() as block:
                def move(eng, done, arr):
                    for c4 in range(QUADS):
                        for q in range(QUADS):
                            for s in range(SIDES):
                                src = raw[32 * c4:32 * c4 + 32, arr, :, QUADS * s + q::M].rearrange(
                                    "t (b i) h -> t h b i", i=NT)
                                dst = cols[32 * q:32 * q + 32, :, arr, s, c4::QUADS].rearrange(
                                    "t (h b) i -> t h b i", b=B)
                                eng(dst, src).then_inc(done, 1)

                @block.vector
                def _(dve):
                    move(dve.tensor_copy, dve_s, 0)

                @block.scalar
                def _(act):
                    move(act.copy, exp_out, 1)

                @block.gpsimd
                def _(pool):
                    move(pool.tensor_copy, exp_in, 2)

                @block.sync
                def _(sp):
                    for done in (dve_s, exp_out, exp_in):
                        sp.wait_ge(done, QUADS * QUADS * SIDES)
                    sp.dma_start(COL_s.rearrange("h b p a s c -> p (h b) (a s c)"),
                                 cols[:, :, :, :, :].rearrange("p n a s c -> p n (a s c)")).then_inc(put, 16)
                    sp.wait_ge(put, 16)
            fresh()

        tables(nc, sems, fresh, c_pos, c_col, om_side, COSF_s, SINF_s, COST_s, SINT_s)


def project(nc, sems, fresh, x, wq, wk, wv, wbt, rho, tri, ones_c, ident, XN_s, raw, KQ_s, KV_s, G_s, EG_s):
    with ExitStack() as ctx:
        def sb(name, shape):
            return ctx.enter_context(nc.sbuf_tensor("proj_" + name, shape, F32))

        def ps(name, shape):
            return ctx.enter_context(nc.psum_tensor("proj_" + name, shape, F32))

        xs = sb("xs", [128, NT, D])
        sq = sb("sq", [128, NT, D])
        stat = sb("stat", [128, NT])
        std = sb("std", [128, NT])
        xT = sb("xT", [128, T])
        qk = sb("qk", [128, 2, NT, H * DK])
        sqq = sb("sqq", [128, 2, H * DK])
        ssq = sb("ssq", [128, 2, NT, H])
        win = sb("win", [128, NT, H, 2 * WIN])
        kv = sb("kv", [128, NT, H, 2 * DK])
        z = sb("z", [128, NT, 2 * HM])
        ez = sb("ez", [128, NT, 2 * HM])
        g = sb("g", [128, NT, HM])
        ex = sb("ex", [128, NT, HM])
        gt, egt = sb("gt", [HM, T]), sb("egt", [HM, T])
        bank = [ps(f"bank{i}", [128, 512]) for i in range(8)]
        (loaded, dve_s, act_s, pool_s, std_in, std_out, xn_done, xt_done, xt_copied, proj, freed_q, freed_k,
         freed_v, freed_z, logs_in, logs_out, g_done, sums, exp_in, exp_out, gt_done, scaled, put, kv_done) = sems[:24]

        DVE_BEFORE, DVE_TILE = 7, 2
        with nc.Fori(0, B) as b:
            with nc.Block() as block:
                @block.sync
                def _(sp):
                    sp.dma_start(xs[:, :, :], x[bass.ds(b, 1)].rearrange("a (i p) d -> p (a i) d", p=128)).then_inc(loaded, 16)
                    sp.wait_ge(xt_copied, 1)
                    sp.dma_start(XN_s[bass.ds(b, 1)].rearrange("a d t -> d (a t)"), xT[:, :]).then_inc(put, 16)
                    n = 1
                    sp.wait_ge(kv_done, 1)
                    for i in range(NT):
                        for c4 in range(QUADS):
                            sp.dma_start(KV_s[:, bass.ds(b, 1), :, QUADS * i + c4, :].rearrange("h a t e -> t (h a) e"),
                                         kv[32 * c4:32 * c4 + 32, i, :, :]).then_inc(put, 16)
                            n += 1
                    sp.wait_ge(gt_done, 2)
                    for h in range(H):
                        sp.dma_start(G_s[h, bass.ds(b, 1)].rearrange("a m t -> (a m) t"), gt[M * h:M * h + M, :]).then_inc(put, 16)
                        sp.dma_start(EG_s[h, bass.ds(b, 1)].rearrange("a m t -> (a m) t"), egt[M * h:M * h + M, :]).then_inc(put, 16)
                        n += 2
                    sp.wait_ge(scaled, 3)
                    for i in range(NT):
                        sp.dma_start(KQ_s[:, bass.ds(b, 1), :, i, :].rearrange("h a p e -> p (h a) e"), win[:, i, :, :]).then_inc(put, 16)
                        n += 1
                    sp.wait_ge(put, 16 * n)

                @block.tensor
                def _(pe):
                    pe.wait_ge(xn_done, 1)
                    for i in range(NT):
                        last = pe.transpose(bank[0][:, 128 * i:128 * i + 128], xs[:, i, :], ident[:, :])
                    last.then_inc(xt_done, 1)
                    for i in range(NT):
                        pe.wait_ge(xt_copied, 1)
                        if i >= 2:
                            pe.wait_ge(freed_q, 2 * (i - 1))
                            pe.wait_ge(freed_k, i - 1)
                            pe.wait_ge(freed_v, i - 1)
                            pe.wait_ge(freed_z, i - 1)
                        lhsT = xT[:, 128 * i:128 * i + 128]
                        o = 4 * (i % 2)
                        pe.matmul(bank[o][:, :], lhsT, wq[:, :], start=True, stop=True)
                        pe.matmul(bank[o + 1][:, :], lhsT, wk[:, :], start=True, stop=True)
                        pe.matmul(bank[o + 2][:, :], lhsT, wv[:, :], start=True, stop=True)
                        pe.matmul(bank[o + 3][:, 0:2 * HM], lhsT, wbt[:, :], start=True, stop=True).then_inc(proj, 1)
                    pe.wait_ge(g_done, 1)
                    pe.wait_ge(freed_q, 2 * NT)
                    pe.wait_ge(freed_k, NT)
                    pe.wait_ge(freed_v, NT)
                    for i in range(NT):
                        pe.matmul(bank[0][:, HM * i:HM * i + HM], tri[:, :], g[:, i, :], start=True, stop=True)
                    for i in range(NT):
                        pe.matmul(bank[1][:, HM * i:HM * i + HM], ones_c[:, :], g[:, i, :], start=True, stop=True)
                    for i in range(NT):
                        last = pe.matmul(bank[2][0:HM, 128 * i:128 * i + 128], g[:, i, :], tri[:, :], start=True, stop=True)
                    last.then_inc(sums, 1)

                @block.scalar
                def _(act):
                    a = Chain(act, act_s)
                    act.wait_ge(std_in, 1)
                    act.activation(std[:, :], std[:, :], ACT.Sqrt).then_inc(std_out, 1)
                    act.wait_ge(xt_done, 1)
                    act.copy(xT[:, :], bank[0][:, :]).then_inc(xt_copied, 1)
                    for i in range(NT):
                        o = 4 * (i % 2)
                        act.wait_ge(proj, i + 1)
                        if i:
                            act.wait_ge(dve_s, DVE_BEFORE + DVE_TILE * i)
                        act.copy(qk[:, 0, i, :], bank[o][:, :]).then_inc(freed_q, 1)
                        act.activation(sqq[:, 0, :], bank[o][:, :], ACT.Square).then_inc(freed_q, 1)
                        act.copy(qk[:, 1, i, :], bank[o + 1][:, :])\
                           .then_inc(act_s, 1)
                        act.activation(sqq[:, 1, :], bank[o + 1][:, :], ACT.Square).then_inc(freed_k, 1)
                        act.copy(kv[:, i, :, DK:], bank[o + 2][:, :].rearrange("p (h d) -> p h d", h=H)).then_inc(freed_v, 1)
                    act.wait_ge(std_in, 2)
                    act.activation(ssq[:, :, :, :], ssq[:, :, :, :], ACT.Sqrt).then_inc(std_out, 1)
                    act.wait_ge(logs_in, 1)
                    act.activation(ez[:, :, :], z[:, :, :], ACT.Exp, scale=-1.0).then_inc(logs_out, 1)
                    act.wait_ge(logs_in, 2)
                    act.activation(z[:, :, 0:HM], ez[:, :, 0:HM], ACT.Ln).then_inc(logs_out, 1)
                    act.activation(g[:, :, :], z[:, :, HM:], ACT.Ln).then_inc(g_done, 1)
                    act.wait_ge(sums, 1)
                    act.copy(gt[:, :], bank[2][0:HM, :]).then_inc(gt_done, 1)
                    act.wait_ge(gt_done, 1)
                    act.activation(egt[:, :], gt[:, :], ACT.Exp).then_inc(gt_done, 1)
                    act.wait_ge(exp_in, 1)
                    act.activation(ex[:, :, :], raw[:, 1, bass.ds(b * NT, NT), :], ACT.Exp).then_inc(exp_out, 1)
                    act.wait_ge(exp_in, 2)
                    act.activation(raw[:, 2, bass.ds(b * NT, NT), :], raw[:, 2, bass.ds(b * NT, NT), :], ACT.Exp).then_inc(exp_out, 1)
                    act.wait_ge(exp_out, 2)

                @block.vector
                def _(dve):
                    v = Chain(dve, dve_s)
                    dve.wait_ge(loaded, 16)
                    v.link(dve.tensor_reduce(stat[:, :], xs[:, :, :], AX_X, ALU.add))
                    v.link(dve.tensor_scalar(stat[:, :], stat[:, :], 1.0 / D, None, ALU.mult))
                    v.link(dve.tensor_tensor(xs[:, :, :], xs[:, :, :], bcast(stat[:, :], 2, D), ALU.subtract))
                    v.link(dve.tensor_tensor(sq[:, :, :], xs[:, :, :], xs[:, :, :], ALU.mult))
                    v.link(dve.tensor_reduce(stat[:, :], sq[:, :, :], AX_X, ALU.add))
                    dve.tensor_scalar(std[:, :], stat[:, :], 1.0 / D, 1e-5, ALU.mult, ALU.add).then_inc(std_in, 1)
                    dve.wait_ge(std_out, 1)
                    v.link(dve.reciprocal(std[:, :], std[:, :]))
                    dve.tensor_tensor(xs[:, :, :], xs[:, :, :], bcast(std[:, :], 2, D), ALU.mult).then_inc(xn_done, 1)
                    v.link(dve.memset(stat[:, :], 0.0))
                    assert v.n == DVE_BEFORE
                    for i in range(NT):
                        o = 4 * (i % 2)
                        dve.wait_ge(proj, i + 1)
                        dve.tensor_copy(z[:, i, :], bank[o + 3][:, 0:2 * HM]).then_inc(freed_z, 1)
                        dve.wait_ge(freed_q, 2 * i + 2)
                        v(dve.tensor_reduce(ssq[:, 0, i, :], sqq[:, 0, :].rearrange("p (h d) -> p h d", h=H), AX_X, ALU.add))
                        dve.wait_ge(freed_k, i + 1)
                        v(dve.tensor_reduce(ssq[:, 1, i, :], sqq[:, 1, :].rearrange("p (h d) -> p h d", h=H), AX_X, ALU.add))
                    v.wait()
                    dve.tensor_scalar(ssq[:, :, :, :], ssq[:, :, :, :], 1e-6, None, ALU.add).then_inc(std_in, 1)
                    dve.wait_ge(freed_z, NT)
                    dve.tensor_scalar(z[:, :, :], z[:, :, :], -CLAMP, None, ALU.max).then_inc(logs_in, 1)
                    dve.wait_ge(std_out, 2)
                    v.link(dve.reciprocal(ssq[:, :, :, :], ssq[:, :, :, :]))
                    v.link(dve.tensor_scalar(ssq[:, 0, :, :], ssq[:, 0, :, :], DK ** -0.5, None, ALU.mult))
                    dve.wait_ge(logs_out, 1)
                    v.link(dve.tensor_scalar(ez[:, :, :], ez[:, :, :], 1.0, None, ALU.add))
                    v.link(dve.reciprocal(z[:, :, HM:], ez[:, :, HM:]))
                    v.link(dve.tensor_tensor(z[:, :, HM:], z[:, :, HM:], bcast(rho[:, :], 1, NT), ALU.mult))
                    dve.tensor_scalar(z[:, :, HM:], z[:, :, HM:], 1e-6, None, ALU.max).then_inc(logs_in, 1)
                    dve.wait_ge(act_s, NT)
                    dve.wait_ge(freed_v, NT)
                    for i in range(NT):
                        last = dve.tensor_tensor(kv[:, i, :, 0:DK], qk[:, 1, i, :].rearrange("p (h d) -> p h d", h=H),
                                                 bcast(ssq[:, 1, i, :], 2, DK), ALU.mult)
                        if i < NT - 1:
                            v(last)
                        else:
                            last.then_inc(kv_done, 1)
                    for i in range(NT):
                        last = dve.tensor_tensor(win[:, i, :, WIN:WIN + DK], qk[:, 0, i, :].rearrange("p (h d) -> p h d", h=H),
                                                 bcast(ssq[:, 0, i, :], 2, DK), ALU.mult)
                    last.then_inc(scaled, 1)
                    dve.wait_ge(sums, 1)
                    dve.wait_ge(logs_out, 2)
                    G = bank[0][:, 0:NT * HM].rearrange("p (i m) -> p i m", i=NT)
                    G_end = bank[1][:, 0:NT * HM].rearrange("p (i m) -> p i m", i=NT)
                    here = bass.ds(b * NT, NT)
                    v.link(dve.scalar_tensor_tensor(out=raw[:, 0, here, :], in0=z[:, :, 0:HM], scalar=-1.0, in1=G,
                                                    op0=ALU.mult, op1=ALU.subtract))
                    dve.tensor_copy(raw[:, 1, here, :], G).then_inc(exp_in, 1)
                    dve.tensor_tensor(raw[:, 2, here, :], raw[:, 0, here, :], G_end, ALU.add).then_inc(exp_in, 1)
                    dve.wait_ge(exp_out, 1)
                    v.link(dve.tensor_scalar(raw[:, 1, here, :], ex[:, :, :], -1.0, None, ALU.mult))

                @block.gpsimd
                def _(pool):
                    pool.wait_ge(kv_done, 1)
                    for i in range(NT):
                        last = pool.tensor_copy(win[:, i, :, 0:DK], kv[:, i, :, 0:DK])
                        last = pool.tensor_copy(win[:, i, :, DK:WIN], kv[:, i, :, 0:HALF])
                    last.then_inc(scaled, 1)
                    pool.wait_ge(scaled, 2)
                    for i in range(NT):
                        last = pool.tensor_copy(win[:, i, :, WIN + DK:], win[:, i, :, WIN:WIN + HALF])
                    last.then_inc(scaled, 1)
            fresh()


def tables(nc, sems, fresh, c_pos, c_col, om_side, COSF_s, SINF_s, COST_s, SINT_s):
    HEADS = 4
    NTOK = SIDES * NC * HALF
    with ExitStack() as ctx:
        def sb(name, shape):
            return ctx.enter_context(nc.sbuf_tensor("tab_" + name, shape, F32))

        pos_c, freq_row = sb("pos_c", [128, NC]), sb("freq_row", [128, HALF])
        col = sb("col", [128, 4])
        pc = sb("pc", [128, HEADS, SIDES, NC])
        om_now = sb("om_now", [128, HEADS, SIDES])
        ang, turns = sb("ang", [128, HEADS, NTOK]), sb("turns", [128, HEADS, NTOK])
        tok, freq = sb("tok", [128, HEADS, 2, NTOK]), sb("freq", [128, HEADS, 2, NTOK])
        loaded, dve_s, reduced, act_s, done, put, turned = sems[:7]
        with nc.Block() as block:
            @block.sync
            def _(sp):
                sp.dma_start(pos_c[:, :], c_pos[:, 0:NC]).then_inc(loaded, 16)
                sp.dma_start(freq_row[:, :], c_pos[:, NC:NC + HALF]).then_inc(loaded, 16)
                sp.dma_start(col[:, :], c_col).then_inc(loaded, 16)
                sp.wait_ge(loaded, 48)
        fresh()
        with nc.Fori(0, H // HEADS) as h4:
            with nc.Block() as block:
                def turn(dve, i):
                    for k in range(2):
                        dve.wait_ge(done, 2 * i + k + 1)
                        dve.transpose(freq[:, i, k].rearrange("p (u t) -> p u t", t=C),
                                      tok[:, i, k].rearrange("p (u j) -> p u j", j=HALF)).then_inc(turned, 1)

                @block.vector
                def _(dve):
                    v = Chain(dve, dve_s)
                    v.link(dve.tensor_copy(om_now[:, :, :], om_side[:, bass.ds(h4 * HEADS, HEADS), :]))
                    for i in range(HEADS):
                        for s in range(SIDES):
                            v(dve.tensor_scalar(pc[:, i, s, :], pos_c[:, :], om_now[:, i, s:s + 1], None, ALU.mult))
                    v.wait()
                    for i in range(HEADS):
                        v.link(dve.tensor_tensor(ang[:, i].rearrange("p (u j) -> p u j", j=HALF),
                                                 bcast(pc[:, i].rearrange("p s c -> p (s c)"), 2, HALF),
                                                 bcast(freq_row[:, :], 1, UNITS), ALU.mult))
                        v.link(dve.tensor_scalar(turns[:, i], ang[:, i], 1.0 / TWO_PI, ROUND, ALU.mult, ALU.add))
                        v.link(dve.tensor_scalar(turns[:, i], turns[:, i], ROUND, None, ALU.subtract))
                        for part in (CW1, CW2, CW3):
                            v.link(dve.scalar_tensor_tensor(out=ang[:, i], in0=turns[:, i], scalar=-part, in1=ang[:, i],
                                                            op0=ALU.mult, op1=ALU.add))
                        dve.tensor_scalar(ang[:, i], ang[:, i], PI, -PI, ALU.min, ALU.max).then_inc(reduced, 1)
                        if i:
                            turn(dve, i - 1)
                    turn(dve, HEADS - 1)

                @block.scalar
                def _(act):
                    for i in range(HEADS):
                        act.wait_ge(reduced, i + 1)
                        act.activation(tok[:, i, 0], ang[:, i], ACT.Sin).then_inc(done, 1)
                        act.activation(turns[:, i], ang[:, i], ACT.Abs).then_inc(act_s, 1)
                        act.wait_ge(act_s, i + 1)
                        act.activation(tok[:, i, 1], turns[:, i], ACT.Sin, scale=-1.0, bias=col[:, 0:1]).then_inc(done, 1)

                @block.sync
                def _(sp):
                    n = 0
                    for i in range(HEADS):
                        here = bass.ds(h4 * HEADS + i, 1)
                        for k, by_token, by_feature in ((0, SINT_s, SINF_s), (1, COST_s, COSF_s)):
                            sp.wait_ge(done, 2 * i + k + 1)
                            sp.dma_start(by_token[here].rearrange("a p s c j -> (a p) (s c j)"), tok[:, i, k]).then_inc(put, 16)
                            sp.wait_ge(turned, 2 * i + k + 1)
                            for q in range(QUADS):
                                sp.dma_start(by_feature[here, q % 2, :, q // 2::2, :].rearrange("a j s t -> (a j) s t"),
                                             freq[32 * q:32 * q + 32, i, k].rearrange("p (s t) -> p s t", s=SIDES)).then_inc(put, 16)
                            n += 1 + QUADS
                    sp.wait_ge(put, 16 * n)
            fresh()


def recurrence(nc, sems, fresh, c_mat, c_small, ident, w_side, w_pair,
               KQ_s, KV_s, G_s, EG_s, COL_s, COSF_s, SINF_s, COST_s, SINT_s, O_s):
    with ExitStack() as ctx:
        def sb(name, shape):
            return ctx.enter_context(nc.sbuf_tensor("run_" + name, shape, F32))

        def ps(name, shape):
            return ctx.enter_context(nc.psum_tensor("run_" + name, shape, F32))

        KB = sb("KB", [128, 2, PAIRS, NC, 2, C])
        Qd = sb("Qd", [128, 2, PAIRS, T])
        XT = sb("XT", [128, 2, SIDES, NC, C])
        PT = sb("PT", [128, 2, SIDES, NC, C])
        KD = sb("KD", [128, 2, SIDES, NC, 2, DK])
        V = sb("V", [128, 2, NC, DV])
        col = sb("col", [128, 2, 3, SIDES, NC])
        decay = sb("decay", [128, 2, PAIRS, NC])
        win = sb("win", [128, NT, 2 * WIN])
        KT = sb("KT", [128, NC, DK])
        KP = sb("KP", [128, 2, PAIRS, T])
        EG = sb("EG", [128, PAIRS, T])
        DB = sb("DB", [128, SIDES, NC, C])
        kqT = sb("kqT", [128, 4, T])
        cosF, sinF = sb("cosF", [128, PAIRS, T]), sb("sinF", [128, PAIRS, T])
        cosT, sinT = sb("cosT", [128, SIDES, NC, HALF]), sb("sinT", [128, SIDES, NC, HALF])
        tmpv = sb("tmpv", [128, PAIRS, 128])
        turned = sb("turned", [128, NC, 2, HALF])
        tmpg = turned[:, :, :, :].rearrange("p c z j -> p (c z j)")[:, 0:PAIRS * 128].rearrange("p (a t) -> p a t", a=PAIRS)
        AT = sb("AT", [128, SIDES, NC, C])
        AL, XL, EL = sb("AL", [128, C, C]), sb("XL", [128, C, C]), sb("EL", [128, C * C // 4])
        below, row_col = sb("below", [128, C]), sb("row_col", [128, 3])
        in_half, sign = row_col[:, 0:2], row_col[:, 2:3]
        colm = sb("colm", [128, SIDES, NC, 2])
        S = sb("S", [128, 2, PAIRS, DV])
        R = sb("R", [128, SIDES, DV])
        W = sb("W", [128, SIDES, 2, DV])
        O2, O = sb("O2", [128, NT, 2, DV]), sb("O", [128, 2, NT, DV])
        RW = [ps(f"RW{s}", [128, 512]) for s in range(SIDES)]
        SB = [ps(f"SB{s}", [128, 512]) for s in range(SIDES)]
        OB = [ps(f"OB{s}", [128, NT, 128]) for s in range(2)]
        prep = [ps(f"prep{s}", [128, 512]) for s in range(2)]

        (l_win, l_gr, l_eg, l_col, l_kv, l_tab, pe_t, act_t, rot_k, rot_q, pe_s, d_ready, d_exp, scored,
         pool_s, dve_s, qd_done, xt_done, kd_done, pe_o, act_o, stored, tab_used) = sems[:23]
        pe_r, dve_r = sems[23:25], sems[25:27]
        pe_w, act_w = sems[27:29], sems[29:31]
        pe_f, dve_f = sems[31:33], sems[33:35]
        l_const, l_tok, kb_done, o_done, l_v, sin_k, w_set, scaled, rot_qv = sems[35:44]
        with nc.Block() as block:
            @block.sync
            def _(sp):
                sp.dma_start(below[:, :], c_mat[3, :, 0:C]).then_inc(l_const, 16)
                sp.dma_start(row_col[:, :], c_mat[3, :, C:C + 3]).then_inc(l_const, 16)
                sp.wait_ge(l_const, 32)

            @block.gpsimd
            def _(pool):
                pool.memset(KB[:, :, :, :, :, :], 0.0).then_inc(pool_s, 1)
                pool.wait_ge(pool_s, 1)

            @block.vector
            def _(dve):
                for s in range(SIDES):
                    dve.memset(RW[s][:, :], 0.0).then_inc(dve_s, 1)
                dve.wait_ge(dve_s, SIDES)
        fresh()

        def emit(n0, odd, steps, preloaded=True, loads_next=True):

            def here(eng, sem, dmas, a):
                if a or not preloaded:
                    eng.wait_ge(sem, 16 * dmas * (a if preloaded else a + 1))

            with nc.Block() as block:
                @block.sync
                def _(sp):
                    def load(n, used):
                        h = n // B
                        if used:
                            sp.wait_ge(pe_t, 4 * used)
                        sp.dma_start(win[:, :, :], KQ_s.rearrange("h b p i e -> (h b) p i e")[bass.ds(n, 1)].rearrange("a p i e -> p (a i) e")).then_inc(l_win, 16)
                        if used:
                            sp.wait_ge(rot_k, NT * used)
                            sp.wait_ge(rot_q, POOL_Q * used)
                            sp.wait_ge(rot_qv, (NT - POOL_Q) * used)
                        for to, table in ((cosF, COSF_s), (sinF, SINF_s)):
                            for e in range(2):
                                for z in range(2):
                                    at = 64 * e + HALF * z
                                    sp.dma_start(to[at:at + HALF], table[bass.ds(h, 1), e].rearrange("a j p t -> (a j) p t")).then_inc(l_tab, 16)
                        if used:
                            sp.wait_ge(scored, 2 * NT * used)
                        for q in range(QUADS):
                            sp.dma_start(DB[32 * q:32 * q + 32].rearrange("p s c i -> p s (c i)"),
                                         G_s.rearrange("h b m t -> (h b) m t")[bass.ds(n, 1), q::QUADS, :].broadcast_to([32, SIDES, T])).then_inc(l_gr, 16)
                        if used:
                            sp.wait_ge(kd_done, used)
                        for q in range(QUADS):
                            sp.dma_start(KT[32 * q:32 * q + 32],
                                         KV_s.rearrange("h b t c e -> (h b) t c e")[bass.ds(n, 1)].rearrange("a t c e -> (a t) c e")[:, :, 0:DK]).then_inc(l_kv, 16)
                        sp.dma_start(cosT[:, :, :, :], COST_s[bass.ds(h, 1)].rearrange("a p s c j -> (a p) s c j")).then_inc(l_tok, 16)
                        sp.dma_start(sinT[:, :, :, :], SINT_s[bass.ds(h, 1)].rearrange("a p s c j -> (a p) s c j")).then_inc(l_tok, 16)
                        if used:
                            sp.wait_ge(qd_done, 2 * used)
                        for e in range(2):
                            sp.dma_start(EG[64 * e:64 * e + 64],
                                         EG_s.rearrange("h b m t -> (h b) m t")[bass.ds(n, 1), e::2, :].broadcast_to([64, PAIRS, T])).then_inc(l_eg, 16)

                    loads = 0
                    if not preloaded:
                        load(0, None)
                        loads += 1
                    prepared = 0
                    for k, (runs, prepares) in enumerate(steps):
                        if prepares:
                            n = n0 + (k + 1)
                            par = (odd + k + 1) % 2
                            if runs and k:
                                sp.wait_ge(pe_o, NC * k)
                            sp.dma_start(col[:, par], COL_s.rearrange("h b p k s c -> (h b) p k s c")[bass.ds(n, 1)].rearrange("a p k s c -> (a p) k s c")).then_inc(l_col, 16)
                            for q in range(QUADS):
                                sp.dma_start(V[32 * q:32 * q + 32, par],
                                             KV_s.rearrange("h b t c e -> (h b) t c e")[bass.ds(n, 1)].rearrange("a t c e -> (a t) c e")[:, :, DK:]).then_inc(l_v, 16)
                            prepared += 1
                            if loads_next:
                                load(n0 + (k + 2), prepared)
                                loads += 1
                        if runs:
                            sp.wait_ge(o_done, k + 1)
                            sp.dma_start(O_s[bass.ds(n0 + k, 1)].rearrange("a (i p) v -> p (a i) v", p=128), O[:, k % 2]).then_inc(stored, 16)
                    if any(r for r, _ in steps):
                        sp.wait_ge(stored, 16 * sum(r for r, _ in steps))
                    if loads_next:
                        for sem, dmas in ((l_win, 1), (l_tab, 8), (l_gr, QUADS), (l_kv, QUADS), (l_tok, 2), (l_eg, 2)):
                            sp.wait_ge(sem, 16 * dmas * loads)
                        sp.wait_ge(l_v, 64 * prepared)
                        sp.wait_ge(l_col, 16 * prepared)

                @block.gpsimd
                def _(pool):
                    g = Chain(pool, pool_s)
                    prepared = 0
                    for k, (runs, prepares) in enumerate(steps):
                        def sum_outputs():
                            pool.wait_ge(act_o, k + 1)
                            pool.tensor_tensor(O[:, k % 2], O2[:, :, 0, :], O2[:, :, 1, :], ALU.add).then_inc(o_done, 1)

                        if not prepares:
                            sum_outputs()
                            continue
                        par = (odd + k + 1) % 2
                        a = prepared
                        here(pool, l_tab, 8, a)
                        pool.wait_ge(act_t, 4 * a + 2)
                        if a:
                            pool.wait_ge(scored, 2 * NT * a)
                        for i in range(DVE_SIN, NT):
                            t = slice(128 * i, 128 * i + 128)
                            pool.tensor_tensor(KP[:, 0, :, t], sinF[:, :, t], bcast(kqT[:, 1, t], 1, PAIRS), ALU.mult).then_inc(sin_k, 1)
                        here(pool, l_gr, QUADS, a)
                        DBc = DB[:, :, :, :].rearrange("p s c i -> p (s c) i")
                        g.link(pool.tensor_tensor(DBc, DBc, bcast(below[:, :], 1, UNITS), ALU.add))
                        pool.wait_ge(l_col, 16 * (a + 1))
                        colc = col[:, par, 0].rearrange("p s c -> p (s c)")
                        pool.tensor_tensor(DBc, DBc, bcast(colc, 2, C), ALU.add).then_inc(d_ready, 1)
                        for i in range(POOL_Q):
                            t = slice(128 * i, 128 * i + 128)
                            if i == 0:
                                pool.wait_ge(act_t, 4 * a + 4)
                            g(pool.tensor_tensor(KP[:, 1, :, t], cosF[:, :, t], bcast(kqT[:, 2, t], 1, PAIRS), ALU.mult))
                            g.link(pool.tensor_tensor(tmpg, sinF[:, :, t], bcast(kqT[:, 3, t], 1, PAIRS), ALU.mult))
                            pool.tensor_tensor(KP[:, 1, :, t], KP[:, 1, :, t], tmpg, ALU.add).then_inc(rot_q, 1)
                            pool.wait_ge(rot_q, POOL_Q * a + i + 1)
                        here(pool, l_tok, 2, a)
                        here(pool, l_kv, QUADS, a)
                        if runs and k:
                            pool.wait_ge(pe_o, NC * k)
                        g(pool.tensor_tensor(colm[:, :, :, :], bcast(col[:, par, 2], 3, 2),
                                             bcast(bcast(in_half, 1, NC), 1, SIDES), ALU.mult))
                        kt = KT[:, :, :].rearrange("p c (z j) -> p c z j", z=2)
                        for s in range(SIDES):
                            plain = KD[:, par, s, :, 1, :]
                            kd = plain.rearrange("p c (z j) -> p c z j", z=2)
                            for z in range(2):
                                g(pool.tensor_tensor(kd[:, :, z, :], kt[:, :, z, :], cosT[:, s], ALU.mult))
                                g(pool.tensor_tensor(turned[:, :, z, :], kt[:, :, z, :], sinT[:, s], ALU.mult))
                            g.wait()
                            g(pool.tensor_tensor(kd[:, :, 0, :], kd[:, :, 0, :], turned[:, :, 1, :], ALU.add))
                            g.link(pool.tensor_tensor(kd[:, :, 1, :], kd[:, :, 1, :], turned[:, :, 0, :], ALU.subtract))
                            g.link(pool.tensor_tensor(KD[:, par, s, :, 0, :], plain, bcast(colm[:, s, :, 0], 2, DK), ALU.mult))
                            last = pool.tensor_tensor(plain, plain, bcast(colm[:, s, :, 1], 2, DK), ALU.mult)
                            if s < SIDES - 1:
                                g.link(last)
                            else:
                                last.then_inc(kd_done, 1)
                        pool.wait_ge(scaled, a + 1)
                        if POOL_Q < NT:
                            pool.wait_ge(rot_qv, (NT - POOL_Q) * (a + 1))
                        pool.tensor_tensor(Qd[:, par], EG[:, :, :], KP[:, 1], ALU.mult).then_inc(qd_done, 1)
                        if runs:
                            sum_outputs()
                        prepared += 1

                @block.scalar
                def _(act):
                    prepared = ran = 0
                    for k, (runs, prepares) in enumerate(steps):
                        a = prepared

                        def transposed(r):
                            act.wait_ge(pe_t, 4 * a + r + 1)
                            if r == 0 and a:
                                act.wait_ge(rot_k, NT * a)
                                act.wait_ge(rot_q, POOL_Q * a)
                                act.wait_ge(rot_qv, (NT - POOL_Q) * a)
                            if r % 2:
                                act.activation(kqT[:, r, :], prep[r % 2][:, :], ACT.Copy, scale=sign).then_inc(act_t, 1)
                            else:
                                act.copy(kqT[:, r, :], prep[r % 2][:, :]).then_inc(act_t, 1)

                        def exponential():
                            act.wait_ge(d_ready, a + 1)
                            act.activation(DB[:, :, :, :], DB[:, :, :, :], ACT.Exp).then_inc(d_exp, 1)

                        def block_k(i):
                            act.wait_ge(rot_k, NT * a + i + 1)
                            if runs and k and i == 0:
                                act.wait_ge(pe_o, NC * k)
                            for e in range(2):
                                rows = slice(64 * e, 64 * e + 64)
                                last = act.copy(KB[rows, (odd + k + 1) % 2, :, 4 * i:4 * i + 4, e, :],
                                                KP[rows, 0, :, 128 * i:128 * i + 128].rearrange("p a (c t) -> p a c t", t=C))
                                last.then_inc(kb_done, 1)

                        def scale_decays():
                            here(act, l_eg, 2, a)
                            act.wait_ge(w_set, a + 1)
                            par = (odd + k + 1) % 2
                            act.copy(decay[:, par], EG[:, :, C - 1::C]).then_inc(qd_done, 1)
                            act.wait_ge(qd_done, 2 * a + 1)
                            for p in range(PAIRS):
                                last = act.activation(EG[:, p], EG[:, p], ACT.Copy, scale=wp[par][:, p:p + 1])
                            last.then_inc(scaled, 1)

                        jobs = []
                        if prepares:
                            jobs = [lambda r=r: transposed(r) for r in range(4)]
                            blocks = [lambda i=i: block_k(i) for i in range(NT)]
                            jobs += blocks[:2] + [exponential] + blocks[2:] + [scale_decays]
                        if not runs:
                            for job in jobs:
                                job()
                        else:
                            for c in range(NC):
                                for s in range(SIDES):
                                    act.wait_ge(pe_w[s], NC * k + c + 1)
                                    act.copy(W[:, s].rearrange("p l v -> p (l v)"), RW[s][:, DV:3 * DV]).then_inc(act_w[s], 1)
                                for _ in range(ACT_PLACES[c] if prepares else 0):
                                    jobs.pop(0)()
                            assert not jobs
                            act.wait_ge(pe_o, NC * (k + 1))
                            if k:
                                act.wait_ge(o_done, k)
                            act.copy(O2[:, :, :, :], OB[k % 2][:, :, :].rearrange("p i (l v) -> p i l v", l=2)).then_inc(act_o, 1)
                        prepared += prepares

                @block.vector
                def _(dve):
                    v = Chain(dve, dve_s)
                    prepared = 0
                    for k, (runs, prepares) in enumerate(steps):
                        a, par, now = prepared, (odd + k + 1) % 2, (odd + k) % 2

                        def rotate_k(i):
                            t = slice(128 * i, 128 * i + 128)
                            if i == 0:
                                here(dve, l_tab, 8, a)
                                dve.wait_ge(act_t, 4 * a + 1)
                            if i:
                                dve.wait_ge(rot_k, NT * a + i)
                            elif a:
                                dve.wait_ge(rot_k, NT * a)
                                dve.wait_ge(rot_qv, (NT - POOL_Q) * a)
                            v.link(dve.tensor_tensor(tmpv[:, :, :], cosF[:, :, t], bcast(kqT[:, 0, t], 1, PAIRS), ALU.mult))
                            if i < DVE_SIN:
                                dve.wait_ge(act_t, 4 * a + 2)
                                v.link(dve.tensor_tensor(KP[:, 0, :, t], sinF[:, :, t], bcast(kqT[:, 1, t], 1, PAIRS), ALU.mult))
                            else:
                                dve.wait_ge(sin_k, (NT - DVE_SIN) * a + i - DVE_SIN + 1)
                            dve.tensor_tensor(KP[:, 0, :, t], KP[:, 0, :, t], tmpv[:, :, :], ALU.add).then_inc(rot_k, 1)

                        def rotate_q(i):
                            t = slice(128 * i, 128 * i + 128)
                            if i == POOL_Q:
                                dve.wait_ge(act_t, 4 * a + 4)
                                dve.wait_ge(rot_k, NT * (a + 1))
                                if a:
                                    dve.wait_ge(qd_done, 2 * a)
                            else:
                                dve.wait_ge(rot_qv, (NT - POOL_Q) * a + i - POOL_Q)
                            v(dve.tensor_tensor(tmpv[:, :, :], cosF[:, :, t], bcast(kqT[:, 2, t], 1, PAIRS), ALU.mult))
                            v.link(dve.tensor_tensor(KP[:, 1, :, t], sinF[:, :, t], bcast(kqT[:, 3, t], 1, PAIRS), ALU.mult))
                            dve.tensor_tensor(KP[:, 1, :, t], KP[:, 1, :, t], tmpv[:, :, :], ALU.add).then_inc(rot_qv, 1)

                        def take_scores(i):
                            dve.wait_ge(pe_s, NT * a + i + 1)
                            if i == 0:
                                dve.wait_ge(d_exp, a + 1)
                                if a:
                                    dve.wait_ge(xt_done, a)
                            chunks = slice(4 * i, 4 * i + 4)
                            scores = prep[i % 2][:, :].rearrange("p (s c z i) -> p s c z i", s=SIDES, c=4, z=2)
                            v(dve.tensor_tensor(AT[:, :, chunks, :], scores[:, :, :, 0, :], DB[:, :, chunks, :], ALU.mult))
                            for s in range(SIDES):
                                last = dve.scalar_tensor_tensor(
                                    out=PT[:, par, s, chunks, :], in0=scores[:, s, :, 1, :], scalar=wq[par][:, s:s + 1],
                                    in1=DB[:, s, chunks, :], op0=ALU.mult, op1=ALU.mult)
                                last.then_inc(scored, 1)

                        def to_lanes():
                            v.wait()
                            v(dve.transpose(AL[:, :, :], AT[:, :, :, :].rearrange("p s c i -> p i (s c)")))
                            v.link(dve.memset(XL[:, :, :], 0.0))
                            v.link(dve.memset(XL[:, :, :].rearrange("p i j -> p (i j)")[:, ::C + 1], 1.0))

                        def eliminate(r):
                            rows, done = C - 1 - r, r + 1
                            e = EL[:, 0:rows * done].rearrange("p (i j) -> p i j", i=rows)
                            v.link(dve.tensor_tensor(e, bcast(AL[:, r + 1:, r], 2, done), bcast(XL[:, r, 0:done], 1, rows), ALU.mult))
                            v.link(dve.tensor_tensor(XL[:, r + 1:, 0:done], XL[:, r + 1:, 0:done], e, ALU.subtract))

                        def from_lanes():
                            dve.transpose(XT[:, par].rearrange("p s c i -> p i (s c)"), XL[:, :, :]).then_inc(xt_done, 1)
                            dve.wait_ge(xt_done, a + 1)

                        def weights():
                            h = (n0 + (k + 1)) // B
                            v.link(dve.tensor_copy(wq[par][:, :], w_side[:, bass.ds(h, 1), :].rearrange("p a s -> p (a s)")))
                            dve.tensor_copy(wp[par][:, :], w_pair[:, bass.ds(h, 1), :].rearrange("p a s -> p (a s)")).then_inc(w_set, 1)

                        jobs = []
                        if prepares:
                            jobs += [weights]
                            jobs += [lambda i=i: rotate_k(i) for i in range(NT)]
                            jobs += [lambda i=i: rotate_q(i) for i in range(POOL_Q, NT)]
                            jobs += [lambda i=i: take_scores(i) for i in range(NT)]
                            rounds = [lambda r=r: eliminate(r) for r in range(C - 1)]
                            jobs += [to_lanes] + rounds + [from_lanes]
                        if not runs:
                            for job in jobs:
                                job()
                        else:
                            plan = DVE_PLACES if prepares else [0] * (2 * NC)
                            for c in range(NC):
                                for s in range(SIDES):
                                    if c:
                                        dve.wait_ge(pe_r[s], (NC - 1) * k + c)
                                        dve.scalar_tensor_tensor(
                                            out=R[:, s, :], in0=RW[s][:, 0:DV], scalar=col[:, now, 1, s, c:c + 1],
                                            in1=V[:, now, c, :], op0=ALU.mult, op1=ALU.add).then_inc(dve_r[s], 1)
                                for _ in range(plan[2 * c]):
                                    jobs.pop(0)()
                                if c < NC - 1:
                                    for s in range(SIDES):
                                        dve.wait_ge(pe_f[s], (NC - 1) * k + c + 1)
                                        if c:
                                            dve.wait_ge(dve_f[s], 2 * ((NC - 1) * k + c))
                                        for p, new in ((2 * s, SB[s][:, 0:DV]), (2 * s + 1, SB[s][:, DV:2 * DV])):
                                            if c == 0:
                                                last = dve.tensor_copy(S[:, (c + 1) % 2, p, :], new)
                                            else:
                                                last = dve.scalar_tensor_tensor(
                                                    out=S[:, (c + 1) % 2, p, :], in0=S[:, c % 2, p, :],
                                                    scalar=decay[:, now, p, c:c + 1], in1=new, op0=ALU.mult, op1=ALU.add)
                                            last.then_inc(dve_f[s], 1)
                                for _ in range(plan[2 * c + 1]):
                                    jobs.pop(0)()
                            assert not jobs, len(jobs)
                        prepared += prepares

                @block.tensor
                def _(pe):
                    prepared = 0
                    for k, (runs, prepares) in enumerate(steps):
                        a, par, now = prepared, (odd + k + 1) % 2, (odd + k) % 2

                        def transposes(r):
                            if r == 0:
                                here(pe, l_win, 1, a)
                            if r < 2:
                                if a:
                                    pe.wait_ge(scored, 2 * (NT * (a - 1) + 3 + r))
                            else:
                                pe.wait_ge(act_t, 4 * a + r - 1)
                            off = WIN * (r // 2) + HALF * (r % 2)
                            for i in range(NT):
                                for e in range(2):
                                    last = pe.matmul(prep[r % 2][64 * e:64 * e + 64, 128 * i:128 * i + 128],
                                                     win[:, i, off:off + DK], ident[:, :], start=True, stop=True)
                            last.then_inc(pe_t, 1)

                        def scores(i, c4):
                            if c4 == 0:
                                pe.wait_ge(kb_done, 2 * (NT * a + i + 1))
                                if i < POOL_Q:
                                    pe.wait_ge(rot_q, POOL_Q * a + i + 1)
                                else:
                                    pe.wait_ge(rot_qv, (NT - POOL_Q) * a + i - POOL_Q + 1)
                                if i < 2:
                                    pe.wait_ge(act_t, 4 * a + 3 + i)
                                else:
                                    pe.wait_ge(scored, 2 * (NT * a + i - 1))
                            c = 4 * i + c4
                            t = slice(C * c, C * c + C)
                            for p in range(PAIRS):
                                s, l = p // 2, p % 2
                                at = 256 * s + 64 * c4
                                last = pe.matmul(prep[i % 2][64 * l:64 * l + 64, at:at + 64],
                                                 KB[:, par, p, c].rearrange("p e t -> p (e t)"), KP[:, :, p, t], start=True, stop=True)
                            if c4 == 3:
                                last.then_inc(pe_s, 1)

                        def read_state(s, c):
                            pe.wait_ge(dve_f[s], 2 * ((NC - 1) * k + c))
                            for l in range(2):
                                p = 2 * s + l
                                last = pe.matmul(RW[s][64 * l:64 * l + 64, 0:DV], KB[:, now, p, c].rearrange("p e t -> p (e t)"),
                                                 S[:, c % 2, p, :], start=True, stop=True)
                            last.then_inc(pe_r[s], 1)

                        def solve(s, c):
                            if c:
                                pe.wait_ge(dve_r[s], (NC - 1) * k + c)
                            elif k:
                                pe.wait_ge(act_w[s], NC * k)
                            for q in range(QUADS):
                                rows = slice(32 * q, 32 * q + 32)
                                rhs = R[rows, s, :] if c else V[rows, now, c, :]
                                at = DV + DV * (q // 2)
                                last = pe.matmul(RW[s][rows, at:at + DV], XT[rows, now, s, c, :], rhs, start=True, stop=True)
                            last.then_inc(pe_w[s], 1)

                        def write_state(s, c):
                            pe.wait_ge(act_w[s], NC * k + c + 1)
                            last = pe.matmul(SB[s][:, 0:2 * DV], KD[:, now, s, c].rearrange("p e k -> p (e k)"),
                                             W[:, s].rearrange("p l v -> p (l v)"), start=True, stop=True)
                            last.then_inc(pe_f[s], 1)

                        def output(c):
                            to = OB[now][32 * (c % 4):32 * (c % 4) + 32, c // 4, :]
                            if c == NC - 1:
                                for s in range(SIDES):
                                    pe.wait_ge(act_w[s], NC * k + c + 1)
                            for s in range(SIDES):
                                last = pe.matmul(to, PT[:, now, s, c, :], W[:, s].rearrange("p l v -> p (l v)"),
                                                 start=(s == 0), stop=(s == 1 and c == 0))
                            if c:
                                for p in range(PAIRS):
                                    last = pe.matmul(to[:, 0:DV], Qd[:, now, p, C * c:C * c + C], S[:, c % 2, p, :],
                                                     start=False, stop=(p == PAIRS - 1))
                            last.then_inc(pe_o, 1)

                        jobs = []
                        if prepares:
                            jobs += [lambda r=r: transposes(r) for r in range(4)]
                            jobs += [lambda i=i, c4=c4: scores(i, c4) for i in range(NT) for c4 in range(4)]
                        if not runs:
                            for job in jobs:
                                job()
                        else:
                            plan = PE_PLACES if prepares else [0] * (2 * NC)
                            for c in range(NC):
                                for s in range(SIDES):
                                    if c:
                                        read_state(s, c)
                                for _ in range(plan[2 * c]):
                                    jobs.pop(0)()
                                for s in range(SIDES):
                                    solve(s, c)
                                for _ in range(plan[2 * c + 1]):
                                    jobs.pop(0)()
                                if c < NC - 1:
                                    for s in range(SIDES):
                                        write_state(s, c)
                                elif prepares and k + 1 < len(steps):
                                    pe.wait_ge(l_v, 64 * (a + 1))
                                output(c)
                            assert not jobs, len(jobs)
                        if prepares and k + 1 < len(steps):
                            pe.wait_ge(xt_done, a + 1)
                            pe.wait_ge(kd_done, a + 1)
                            pe.wait_ge(qd_done, 2 * (a + 1))
                            pe.wait_ge(scored, 2 * NT * (a + 1))
                        prepared += prepares
            fresh()

        wq = [sb(f"wq_{p}", [128, SIDES]) for p in range(2)]
        wp = [sb(f"wp_{p}", [128, PAIRS]) for p in range(2)]
        PE_PLACES = [0, 2, 0, 2, 0, 0, 0, 0, 2, 2, 2, 2, 2, 2, 2, 2, 0, 0, 0, 0, 0, 0, 0, 0, 0, 0, 0, 0, 0, 0, 0, 0]
        DVE_PLACES = [0, 0, 2, 0, 1, 0, 1, 0, 1, 1, 1, 0, 1, 0, 1, 0, 1, 4, 2, 2, 3, 2, 2, 2, 3, 2, 2, 3, 2, 2, 1, 1]
        ACT_PLACES = [2, 2, 1, 1, 2, 1, 0, 0, 1, 0, 0, 0, 0, 0, 0, 0]

        emit(-1, 1, [(False, True)], preloaded=False)
        with nc.Fori(0, NSEQ // 2 - 1) as r:
            emit(r * 2, 0, [(True, True), (True, True)])
        emit(NSEQ - 2, 0, [(True, True), (True, False)], loads_next=False)


def experts(nc, sems, fresh, x, Wg, Wo, gate_w, w13, w2, c_small, ident, XN_s, O_s, out):
    KT = H * DV // 128
    IC = 2 * INTER // 128
    with ExitStack() as ctx:
        def sb(name, shape):
            return ctx.enter_context(nc.sbuf_tensor("moe_" + name, shape, F32))

        def ps(name, shape):
            return ctx.enter_context(nc.psum_tensor("moe_" + name, shape, F32))

        wg, wo = sb("wg", [128, H * DV]), sb("wo", [128, KT, D])
        gw, gwT = sb("gw", [E_X, D]), sb("gwT", [D, E_X])
        w13T = sb("w13T", [D, E_X, IC, 128])
        w2T = sb("w2T", [128, E_X, INTER // 128, D])
        earlier = sb("earlier", [128, E_X, E_X])
        earlier_g = sb("earlier_g", [128, GROUPS, GROUPS])
        bank = [ps(f"ebank{i}", [128, 512]) for i in range(8)]
        sm = sems
        with ExitStack() as part:
            nat13 = part.enter_context(nc.sbuf_tensor("nat13", [128, E_X, IC, D], F32))
            nat2 = part.enter_context(nc.sbuf_tensor("nat2", [D, E_X, INTER], F32))
            loaded, turned, copied = sm[:3]
            with nc.Block() as block:
                @block.sync
                def _(sp):
                    sp.dma_start(wg[:, :], Wg).then_inc(loaded, 16)
                    sp.dma_start(wo[:, :, :], Wo.rearrange("(k p) n -> p k n", p=128)).then_inc(loaded, 16)
                    sp.dma_start(gw[:, :], gate_w).then_inc(loaded, 16)
                    sp.dma_start(nat13[:, :, :, :], w13.rearrange("e (i p) d -> p e i d", p=128)).then_inc(loaded, 16)
                    sp.dma_start(nat2[:, :, :], w2.rearrange("e d i -> d e i")).then_inc(loaded, 16)
                    sp.dma_start(earlier[:, :, :].rearrange("p a b -> p (a b)"),
                                 c_small[1:2, 0:64].broadcast_to([128, 64])).then_inc(loaded, 16)
                    sp.dma_start(earlier_g[:, :, :].rearrange("p a b -> p (a b)"),
                                 c_small[1:2, 64:80].broadcast_to([128, 16])).then_inc(loaded, 16)
                    sp.wait_ge(loaded, 7 * 16)

                @block.tensor
                def _(pe):
                    pe.wait_ge(loaded, 7 * 16)
                    pe.transpose(bank[0][:, 0:E_X], gw[:, :], ident[0:E_X, 0:E_X]).then_inc(turned, 1)
                    for e in range(E_X):
                        if e:
                            pe.wait_ge(copied, 1 + 2 * e)
                        for i in range(IC):
                            last = pe.transpose(bank[1][:, 128 * i:128 * i + 128], nat13[:, e, i, :], ident[:, :])
                        last.then_inc(turned, 1)
                        for i in range(INTER // 128):
                            last = pe.transpose(bank[2][:, 128 * i:128 * i + 128], nat2[:, e, 128 * i:128 * i + 128], ident[:, :])
                        last.then_inc(turned, 1)

                @block.vector
                def _(dve):
                    dve.wait_ge(turned, 1)
                    dve.tensor_copy(gwT[:, :], bank[0][:, 0:E_X]).then_inc(copied, 1)
                    for e in range(E_X):
                        dve.wait_ge(turned, 2 + 2 * e)
                        dve.tensor_copy(w13T[:, e, :, :].rearrange("p i k -> p (i k)"), bank[1][:, :]).then_inc(copied, 1)
                        dve.wait_ge(turned, 3 + 2 * e)
                        dve.tensor_copy(w2T[:, e, :, :].rearrange("p i k -> p (i k)"), bank[2][:, 0:INTER]).then_inc(copied, 1)
            fresh()

        o = sb("o", [128, NT, H * DV])
        gate = sb("gate", [128, NT, H * DV])
        xs = sb("exs", [128, NT, D])
        xT = sb("exT", [128, T])
        oT = sb("oT", [128, KT, T])
        x1 = sb("x1", [128, NT, D])
        xn = sb("exn", [128, NT, D])
        sq = sb("esq", [128, NT, D])
        stat, std = sb("estat", [128, NT]), sb("estd", [128, NT])
        x2T = sb("x2T", [D, T])
        sc = sb("sc", [128, NT, E_X])
        red = sb("red", [128, NT])
        grp = sb("grp", [128, NT, GROUPS])
        cg, cg2 = sb("cg", [128, NT, GROUPS, GROUPS]), sb("cg2", [128, NT, GROUPS, GROUPS])
        ce, ce2 = sb("ce", [128, NT, E_X, E_X]), sb("ce2", [128, NT, E_X, E_X])
        rank_g, rank = sb("rank_g", [128, NT, GROUPS]), sb("rank", [128, NT, E_X])
        comb = sb("comb", [128, NT, E_X])
        sil = sb("sil", [128, 2, T])
        hid = sb("hid", [128, 2, 2, T])
        acc = sb("acc", [128, NT, D])
        (l_x, l_o, xt_in, pe_g, sig, gated, pe_to, oT_s, pe_y, dve_s, std_in, std_out, xn_in, pe_x2, x2_s, pe_sc,
         e_in, e_out, pe_h, act_h, dve_h, pe_z, dve_z, stored, gate_f) = sm[:25]
        with nc.Fori(0, B) as b:
            with nc.Block() as block:
                @block.sync
                def _(sp):
                    sp.dma_start(xs[:, :, :], x[bass.ds(b, 1)].rearrange("a (i p) d -> p (a i) d", p=128)).then_inc(l_x, 16)
                    sp.dma_start(xT[:, :], XN_s[bass.ds(b, 1)].rearrange("a d t -> d (a t)")).then_inc(xt_in, 16)
                    for i in range(NT):
                        sp.dma_start(o[:, i, :].rearrange("p (h v) -> p h v", h=H),
                                     O_s.rearrange("(h b) (i p) v -> h b i p v", b=B, p=128)[:, bass.ds(b, 1), i].rearrange("h a p v -> p (h a) v")).then_inc(l_o, 16)
                    sp.wait_ge(dve_z, E_X * NT)
                    sp.dma_start(out[bass.ds(b, 1)].rearrange("a (i p) d -> p (a i) d", p=128), acc[:, :, :]).then_inc(stored, 16)
                    sp.wait_ge(stored, 16)

                @block.tensor
                def _(pe):
                    pe.wait_ge(xt_in, 16)
                    for i in range(NT):
                        pe.matmul(bank[i][:, :], xT[:, 128 * i:128 * i + 128], wg[:, :], start=True, stop=True).then_inc(pe_g, 1)
                    for k in range(KT):
                        for i in range(NT):
                            pe.wait_ge(gated, i + 1)
                            last = pe.transpose(bank[4 + k][:, 128 * i:128 * i + 128], o[:, i, 128 * k:128 * k + 128], ident[:, :])
                        last.then_inc(pe_to, 1)
                    pe.wait_ge(oT_s, KT)
                    for i in range(NT):
                        for k in range(KT):
                            last = pe.matmul(bank[0][:, D * i:D * i + D], oT[:, k, 128 * i:128 * i + 128], wo[:, k, :],
                                             start=(k == 0), stop=(k == KT - 1))
                    last.then_inc(pe_y, 1)
                    pe.wait_ge(xn_in, 1)
                    for i in range(NT):
                        last = pe.transpose(bank[1][:, 128 * i:128 * i + 128], xn[:, i, :], ident[:, :])
                    last.then_inc(pe_x2, 1)
                    pe.wait_ge(x2_s, 1)
                    for i in range(NT):
                        last = pe.matmul(bank[2][:, E_X * i:E_X * i + E_X], x2T[:, 128 * i:128 * i + 128], gwT[:, :], start=True, stop=True)
                    last.then_inc(pe_sc, 1)

                    def up(e):
                        for j in range(2):
                            if e == 0 and j == 0:
                                pe.wait_ge(e_in, 1)
                            if e:
                                pe.wait_ge(dve_h, 2 * (e - 1) + j + 1)
                            pe.matmul(bank[2 + 2 * j][:, :], w13T[:, e, j, :], x2T[:, :], start=True, stop=True)
                            pe.matmul(bank[3 + 2 * j][:, :], w13T[:, e, 2 + j, :], x2T[:, :], start=True, stop=True).then_inc(pe_h, 1)

                    def down(e):
                        pe.wait_ge(dve_h, 2 * e + 2)
                        if e >= 2:
                            pe.wait_ge(dve_z, NT * (e - 1))
                        for i in range(NT):
                            for j in range(2):
                                last = pe.matmul(bank[6 + e % 2][:, D * i:D * i + D], hid[:, e % 2, j, 128 * i:128 * i + 128],
                                                 w2T[:, e, j, :], start=(j == 0), stop=(j == 1))
                        last.then_inc(pe_z, 1)

                    up(0)
                    for e in range(E_X):
                        if e + 1 < E_X:
                            up(e + 1)
                        down(e)

                @block.scalar
                def _(act):
                    for i in range(NT):
                        act.wait_ge(pe_g, i + 1)
                        act.activation(gate[:, i, :], bank[i][:, :], ACT.Sigmoid).then_inc(sig, 1)
                    for k in range(KT):
                        act.wait_ge(pe_to, k + 1)
                        act.copy(oT[:, k, :], bank[4 + k][:, :]).then_inc(oT_s, 1)
                    act.wait_ge(std_in, 1)
                    act.activation(std[:, :], std[:, :], ACT.Sqrt).then_inc(std_out, 1)
                    act.wait_ge(pe_x2, 1)
                    act.copy(x2T[:, :], bank[1][:, :]).then_inc(x2_s, 1)
                    act.wait_ge(e_in, 1)
                    act.activation(sc[:, :, :], sc[:, :, :], ACT.Exp).then_inc(e_out, 1)
                    for e in range(E_X):
                        for j in range(2):
                            act.wait_ge(pe_h, 2 * e + j + 1)
                            if e:
                                act.wait_ge(dve_h, 2 * (e - 1) + j + 1)
                            act.activation(sil[:, j, :], bank[2 + 2 * j][:, :], ACT.Silu).then_inc(act_h, 1)

                @block.vector
                def _(dve):
                    v = Chain(dve, dve_s)
                    for i in range(NT):
                        dve.wait_ge(sig, i + 1)
                        dve.wait_ge(l_o, 16 * NT)
                        dve.tensor_tensor(o[:, i, :], o[:, i, :], gate[:, i, :], ALU.mult).then_inc(gated, 1)
                    dve.wait_ge(pe_y, 1)
                    dve.wait_ge(l_x, 16)
                    x1v = x1[:, :, :].rearrange("p i d -> p (i d)")
                    v.link(dve.tensor_tensor(x1v, xs[:, :, :].rearrange("p i d -> p (i d)"), bank[0][:, :], ALU.add))
                    v.link(dve.tensor_reduce(stat[:, :], x1[:, :, :], AX_X, ALU.add))
                    v.link(dve.tensor_scalar(stat[:, :], stat[:, :], 1.0 / D, None, ALU.mult))
                    v.link(dve.tensor_tensor(xn[:, :, :], x1[:, :, :], bcast(stat[:, :], 2, D), ALU.subtract))
                    v.link(dve.tensor_tensor(sq[:, :, :], xn[:, :, :], xn[:, :, :], ALU.mult))
                    v.link(dve.tensor_reduce(stat[:, :], sq[:, :, :], AX_X, ALU.add))
                    dve.tensor_scalar(std[:, :], stat[:, :], 1.0 / D, 1e-5, ALU.mult, ALU.add).then_inc(std_in, 1)
                    dve.wait_ge(std_out, 1)
                    v.link(dve.reciprocal(std[:, :], std[:, :]))
                    dve.tensor_tensor(xn[:, :, :], xn[:, :, :], bcast(std[:, :], 2, D), ALU.mult).then_inc(xn_in, 1)
                    dve.wait_ge(pe_sc, 1)
                    raw = bank[2][:, 0:NT * E_X].rearrange("p (i e) -> p i e", i=NT)
                    v.link(dve.tensor_reduce(red[:, :], raw, AX_X, ALU.max))
                    dve.tensor_tensor(sc[:, :, :], raw, bcast(red[:, :], 2, E_X), ALU.subtract).then_inc(e_in, 1)
                    dve.wait_ge(e_out, 1)
                    v.link(dve.tensor_reduce(red[:, :], sc[:, :, :], AX_X, ALU.add))
                    v.link(dve.reciprocal(red[:, :], red[:, :]))
                    v.link(dve.tensor_tensor(sc[:, :, :], sc[:, :, :], bcast(red[:, :], 2, E_X), ALU.mult))
                    per = E_X // GROUPS
                    v.link(dve.tensor_tensor(grp[:, :, :], sc[:, :, 0::per], sc[:, :, 1::per], ALU.max))

                    def ranks(values, n, to, one, two, first_wins):
                        for i in range(NT):
                            other = bcast(values[:, i, :], 1, n)
                            own = bcast(values[:, i, :], 2, n)
                            v(dve.tensor_tensor(one[:, i], other, own, ALU.is_equal))
                            v(dve.tensor_tensor(two[:, i], other, own, ALU.is_gt))
                        v.wait()
                        for i in range(NT):
                            v(dve.tensor_tensor(one[:, i], one[:, i], first_wins[:, :, :], ALU.mult))
                        v.wait()
                        v.link(dve.tensor_tensor(one[:, :, :, :], one[:, :, :, :], two[:, :, :, :], ALU.add))
                        v.link(dve.tensor_reduce(to[:, :, :], one[:, :, :, :], AX_X, ALU.add))

                    ranks(grp, GROUPS, rank_g, cg, cg2, earlier_g)
                    v.link(dve.tensor_scalar(rank_g[:, :, :], rank_g[:, :, :], 2.0, None, ALU.is_lt))
                    for j in range(per):
                        v(dve.tensor_tensor(sc[:, :, j::per], sc[:, :, j::per], rank_g[:, :, :], ALU.mult))
                    v.wait()
                    ranks(sc, E_X, rank, ce, ce2, earlier)
                    v.link(dve.tensor_scalar(rank[:, :, :], rank[:, :, :], 2.0, None, ALU.is_lt))
                    v.link(dve.tensor_tensor(comb[:, :, :], sc[:, :, :], rank[:, :, :], ALU.mult))
                    v.link(dve.tensor_reduce(red[:, :], comb[:, :, :], AX_X, ALU.add))
                    v.link(dve.reciprocal(red[:, :], red[:, :]))
                    v.link(dve.tensor_tensor(comb[:, :, :], comb[:, :, :], bcast(red[:, :], 2, E_X), ALU.mult))

                    def hidden(e):
                        for j in range(2):
                            dve.wait_ge(act_h, 2 * e + j + 1)
                            if e >= 2:
                                dve.wait_ge(pe_z, e - 1)
                            dve.tensor_tensor(hid[:, e % 2, j, :], sil[:, j, :], bank[3 + 2 * j][:, :], ALU.mult).then_inc(dve_h, 1)

                    def add(e):
                        dve.wait_ge(pe_z, e + 1)
                        if e:
                            dve.wait_ge(dve_z, NT * e)
                        for i in range(NT):
                            dve.scalar_tensor_tensor(out=acc[:, i, :], in0=bank[6 + e % 2][:, D * i:D * i + D],
                                                     scalar=comb[:, i, e:e + 1], in1=acc[:, i, :] if e else x1[:, i, :],
                                                     op0=ALU.mult, op1=ALU.add).then_inc(dve_z, 1)

                    hidden(0)
                    for e in range(E_X):
                        if e + 1 < E_X:
                            hidden(e + 1)
                        add(e)
            fresh()


_INS = ["L0_attn_hidden_states", "L0_attn_Wq", "L0_attn_Wk", "L0_attn_Wv", "L0_attn_Wbeta", "L0_attn_Wtg",
        "L0_attn_mode_logits", "L0_attn_log_decay", "L0_attn_omega_log_scale", "L0_attn_Wg", "L0_attn_Wo",
        "L0_ffn_gate_w", "L0_ffn_w13_weight", "L0_ffn_w2_weight"]


def _constants(np):
    f = np.float32
    at = np.arange(128)
    same = (at[:, None] // C) == (at[None, :] // C)
    mat = np.zeros((4, 128, 128), f)
    mat[0] = np.eye(128)
    mat[1] = same & (at[:, None] <= at[None, :])
    mat[2] = same
    mat[3, :, C + 2] = np.where(at % DK < HALF, 1.0, -1.0)
    mat[3, :, C:C + 2] = (at // C % 2)[:, None] == np.arange(2)[None, :]
    mat[3, :, 0:C] = np.where((at % C)[:, None] <= np.arange(C)[None, :], 0.0, -1e30)
    freq = (f(1.0) / f(10000.0) ** (np.arange(0, DK, 2, dtype=f) / f(DK))).astype(f)
    pos = np.zeros((128, NC + HALF), f)
    pos[:, 0:NC] = (at % C)[:, None] + C * np.arange(NC)[None, :]
    pos[:, NC:] = freq
    col = np.full((128, 4), np.pi / 2, f)
    small = np.zeros((2, C * C), f)
    small[1, 0:64] = (np.arange(E_X)[None, :] < np.arange(E_X)[:, None]).reshape(-1)
    small[1, 64:80] = (np.arange(GROUPS)[None, :] < np.arange(GROUPS)[:, None]).reshape(-1)
    return {"c_mat": mat, "c_pos": pos, "c_col": col, "c_small": small}


def kernel(**inputs):
    import numpy as _np
    import concourse.bacc as _bacc
    from concourse.bass_utils import run_bass_kernel_spmd as _run

    nc = _bacc.Bacc("TRN2", target_bir_lowering=False, num_devices=1)
    arrays, args = {}, []
    given = {name: _np.ascontiguousarray(inputs[name]) for name in _INS}
    for name, a in {**given, **_constants(_np)}.items():
        arrays[f"in_{name}_dram"] = a
        args.append(nc.dram_tensor(f"in_{name}_dram", a.shape, mybir.dt.from_np(a.dtype), kind="ExternalInput").ap())
    out = nc.dram_tensor("out_0_dram", (B, T, D), F32, kind="ExternalOutput").ap()
    program(nc, *args, out)
    r = _run(nc, [arrays], core_ids=[0])
    return r.results[0]["out_0_dram"]
```
